# Optimizing a Trainium2 kernel written in Bass

```python
import numpy as np
import jax
import jax.numpy as jnp

def _softmax(x, axis=-1):
    return jax.nn.softmax(x, axis=axis)

def _gelu(x):
    return jax.nn.gelu(x, approximate=True)

def _silu(x):
    return jax.nn.silu(x)

def _sigmoid(x):
    return jax.nn.sigmoid(x)

def _layernorm(x, axis=-1, eps=1e-05):
    m = jnp.mean(x, axis=axis, keepdims=True)
    v = jnp.var(x, axis=axis, keepdims=True)
    return (x - m) / jnp.sqrt(v + eps)

def _scatter_add(tgt, idx, src, axis=0):
    return tgt.at[idx].add(src)

def _segment_sum(src, seg, n):
    return jax.ops.segment_sum(src, seg, n)
kernel_name = 'mk_adj_preln_d4_adj_r2_236833'

def setup_inputs(seed: int=0):
    np.random.seed(seed)
    _w = jnp.asarray

    def _rec_inputs():
        import jax
        import jax.numpy as jnp
        _gk = jax.random.key(seed)
        x = -0.0005207 + 1.001 * jax.random.normal(jax.random.fold_in(_gk, 1), (2048, 128), jnp.float32)
        _w = (1.0 + jnp.arange(2048, dtype=jnp.float32)) ** (-0.5)
        _w = _w / _w.mean()
        _pij = jnp.clip(0.00195312 * _w[:, None] * _w[None, :], 0.0, 1.0)
        _a = jax.random.uniform(jax.random.fold_in(_gk, 2), (2048, 2048)) < _pij
        _a = jnp.logical_or(_a, jnp.eye(2048, dtype=bool))
        _af = _a.astype(jnp.float32)
        _af = _af * jax.random.uniform(jax.random.fold_in(_gk, 3), (2048, 2048), jnp.float32, 0.05, 1)
        adj = _af
        return (x, adj)
    x, adj = _rec_inputs()

    def _L0_gnn_setup():
        import jax, jax.numpy as jnp
        import numpy as np
        THRESH = 1e-06
        EPS = 1e-08
        LN_EPS = 1e-05

        def _layer(h, M, W_in, b_in, W_out, b_out, W_self, b_self, gamma, beta):
            A = M / (jnp.sum(M, axis=0, keepdims=True) + EPS)
            mask = A > THRESH
            W = jnp.where(mask, A, 0.0)
            T = h @ W_in + b_in
            weighted_sum = jnp.einsum('ji,jd->id', W, T)
            weight_sum = jnp.sum(W, axis=0)
            has_edge = jnp.any(mask, axis=0)
            agg = jnp.where(has_edge[:, None], weighted_sum / (weight_sum[:, None] + EPS), T)
            agg = agg @ W_out + b_out
            out = agg + (h @ W_self + b_self)
            mu = jnp.mean(out, axis=-1, keepdims=True)
            var = jnp.mean(jnp.square(out - mu), axis=-1, keepdims=True)
            out = (out - mu) * jax.lax.rsqrt(var + LN_EPS) * gamma + beta
            return out
        key = jax.random.key(seed)
        ks = jax.random.split(key, 16)
        N, D_IN, D_H, D_OUT = (4096, 128, 256, 128)
        s = 0.05
        return {'node_features': jax.random.normal(ks[0], (N, D_IN), jnp.float32), 'mobility_matrix': jax.random.uniform(ks[1], (N, N), jnp.float32), 'W_in1': jax.random.normal(ks[2], (D_IN, D_H)) * s, 'b_in1': jnp.zeros((D_H,)), 'W_out1': jax.random.normal(ks[3], (D_H, D_H)) * s, 'b_out1': jnp.zeros((D_H,)), 'W_self1': jax.random.normal(ks[4], (D_IN, D_H)) * s, 'b_self1': jnp.zeros((D_H,)), 'g1': jnp.ones((D_H,)), 'be1': jnp.zeros((D_H,)), 'W_in2': jax.random.normal(ks[5], (D_H, D_OUT)) * s, 'b_in2': jnp.zeros((D_OUT,)), 'W_out2': jax.random.normal(ks[6], (D_OUT, D_OUT)) * s, 'b_out2': jnp.zeros((D_OUT,)), 'W_self2': jax.random.normal(ks[7], (D_H, D_OUT)) * s, 'b_self2': jnp.zeros((D_OUT,)), 'g2': jnp.ones((D_OUT,)), 'be2': jnp.zeros((D_OUT,))}
    _L0_gnn_all = _L0_gnn_setup()
    _L0_gnn_in = {k: v for k, v in _L0_gnn_all.items() if k in ('W_in1', 'b_in1', 'W_out1', 'b_out1', 'W_self1', 'b_self1', 'g1', 'be1', 'W_in2', 'b_in2', 'W_out2', 'b_out2', 'W_self2', 'b_self2', 'g2', 'be2')}
    del _L0_gnn_all

    def _L1_gnn_setup():
        import jax, jax.numpy as jnp
        import numpy as np
        N = 10000
        D = 128
        F = 128
        K = F // 8
        key = jax.random.key(seed)
        k1, k2, k3, k4, k5 = jax.random.split(key, 5)
        h = jax.random.normal(k1, (N, D), dtype=jnp.float32)
        adj = jax.random.uniform(k2, (N, N), dtype=jnp.float32)
        W1 = jax.random.normal(k3, (D, K), dtype=jnp.float32) * 0.05
        W2 = jax.random.normal(k4, (K, D, F), dtype=jnp.float32) * 0.05
        b = jax.random.normal(k5, (K, F), dtype=jnp.float32) * 0.05
        return {'h': h, 'adj': adj, 'W1': W1, 'W2': W2, 'b': b}
    _L1_gnn_all = _L1_gnn_setup()
    _L1_gnn_in = {k: v for k, v in _L1_gnn_all.items() if k in ('W1', 'W2', 'b')}
    del _L1_gnn_all

    def _L2_gnn_setup():
        import jax, jax.numpy as jnp
        import numpy as np
        D_IN = 128
        D_ATTN = 64
        STEPS = 2
        TOP_P = 0.9
        TAU = 1.0
        LN_EPS = 1e-05
        N_NODES = 4096

        def _top_p_attention(X, W1, W2, W3):
            q = X @ W1.T @ W2.T
            k = X @ W3.T
            logits = q @ k.T / TAU
            probs = jax.nn.softmax(logits, axis=-1)
            idx = jnp.argsort(-probs, axis=-1)
            sp = jnp.take_along_axis(probs, idx, axis=-1)
            cs = jnp.cumsum(sp, axis=-1)
            keep_sorted = cs - sp < TOP_P
            rows = jnp.arange(probs.shape[0])[:, None]
            mask = jnp.zeros(probs.shape, dtype=bool).at[rows, idx].set(keep_sorted)
            A = probs * mask
            return A / jnp.maximum(A.sum(-1, keepdims=True), 1e-12)
        key = jax.random.key(seed)
        ks = jax.random.split(key, 8)
        N, d, da, steps = (N_NODES, D_IN, D_ATTN, STEPS)
        X = jax.random.normal(ks[0], (N, d), dtype=jnp.float32)
        S = jax.random.uniform(ks[1], (N, N), dtype=jnp.float32)
        W1 = jax.random.normal(ks[2], (da, d), dtype=jnp.float32) / np.sqrt(d)
        W2 = jax.random.normal(ks[3], (da, da), dtype=jnp.float32) / np.sqrt(da)
        W3 = jax.random.normal(ks[4], (da, d), dtype=jnp.float32) / np.sqrt(d)
        U1 = jax.random.normal(ks[5], (steps, d, d), dtype=jnp.float32) / np.sqrt(d)
        U2 = jax.random.normal(ks[6], (steps, d, d), dtype=jnp.float32) / np.sqrt(d)
        ln_g = jnp.ones((d,), dtype=jnp.float32)
        ln_b = jnp.zeros((d,), dtype=jnp.float32)
        return {'X': X, 'S': S, 'W1': W1, 'W2': W2, 'W3': W3, 'U1': U1, 'U2': U2, 'ln_g': ln_g, 'ln_b': ln_b}
    _L2_gnn_all = _L2_gnn_setup()
    _L2_gnn_in = {k: v for k, v in _L2_gnn_all.items() if k in ('W1', 'W2', 'W3', 'U1', 'U2', 'ln_g', 'ln_b')}
    del _L2_gnn_all

    def _L3_gnn_setup():
        import jax, jax.numpy as jnp
        import numpy as np
        N = 4096
        D = 128
        CUTOFF = 1.0
        MU = 1.0
        SIGMA = 0.5

        def sensitivity(r, mu, sigma):
            return jnp.exp(-(1.0 / r - 1.0 / mu) ** 2 / (2.0 * sigma * sigma))
        key = jax.random.key(seed)
        k_z, k_d, k_w = jax.random.split(key, 3)
        z = jax.random.normal(k_z, (N, D), dtype=jnp.float32)
        dist_matrix = jax.random.uniform(k_d, (N, N), dtype=jnp.float32) * 2.0 + 0.05
        W = jax.random.normal(k_w, (D, D), dtype=jnp.float32)
        B = jnp.zeros((D,), dtype=jnp.float32)
        return {'z': z, 'dist_matrix': dist_matrix, 'W': W, 'B': B}
    _L3_gnn_all = _L3_gnn_setup()
    _L3_gnn_in = {k: v for k, v in _L3_gnn_all.items() if k in ('W', 'B')}
    del _L3_gnn_all
    return {'x': x, 'adj': adj, 'L0_gnn_W_in1': _L0_gnn_in['W_in1'], 'L0_gnn_b_in1': _L0_gnn_in['b_in1'], 'L0_gnn_W_out1': _L0_gnn_in['W_out1'], 'L0_gnn_b_out1': _L0_gnn_in['b_out1'], 'L0_gnn_W_self1': _L0_gnn_in['W_self1'], 'L0_gnn_b_self1': _L0_gnn_in['b_self1'], 'L0_gnn_g1': _L0_gnn_in['g1'], 'L0_gnn_be1': _L0_gnn_in['be1'], 'L0_gnn_W_in2': _L0_gnn_in['W_in2'], 'L0_gnn_b_in2': _L0_gnn_in['b_in2'], 'L0_gnn_W_out2': _L0_gnn_in['W_out2'], 'L0_gnn_b_out2': _L0_gnn_in['b_out2'], 'L0_gnn_W_self2': _L0_gnn_in['W_self2'], 'L0_gnn_b_self2': _L0_gnn_in['b_self2'], 'L0_gnn_g2': _L0_gnn_in['g2'], 'L0_gnn_be2': _L0_gnn_in['be2'], 'L1_gnn_W1': _L1_gnn_in['W1'], 'L1_gnn_W2': _L1_gnn_in['W2'], 'L1_gnn_b': _L1_gnn_in['b'], 'L2_gnn_W1': _L2_gnn_in['W1'], 'L2_gnn_W2': _L2_gnn_in['W2'], 'L2_gnn_W3': _L2_gnn_in['W3'], 'L2_gnn_U1': _L2_gnn_in['U1'], 'L2_gnn_U2': _L2_gnn_in['U2'], 'L2_gnn_ln_g': _L2_gnn_in['ln_g'], 'L2_gnn_ln_b': _L2_gnn_in['ln_b'], 'L3_gnn_W': _L3_gnn_in['W'], 'L3_gnn_B': _L3_gnn_in['B']}

def reference(x, adj, L0_gnn_W_in1, L0_gnn_b_in1, L0_gnn_W_out1, L0_gnn_b_out1, L0_gnn_W_self1, L0_gnn_b_self1, L0_gnn_g1, L0_gnn_be1, L0_gnn_W_in2, L0_gnn_b_in2, L0_gnn_W_out2, L0_gnn_b_out2, L0_gnn_W_self2, L0_gnn_b_self2, L0_gnn_g2, L0_gnn_be2, L1_gnn_W1, L1_gnn_W2, L1_gnn_b, L2_gnn_W1, L2_gnn_W2, L2_gnn_W3, L2_gnn_U1, L2_gnn_U2, L2_gnn_ln_g, L2_gnn_ln_b, L3_gnn_W, L3_gnn_B):
    import jax
    import jax.numpy as jnp

    def _L0_gnn_ref(node_features, mobility_matrix, W_in1, b_in1, W_out1, b_out1, W_self1, b_self1, g1, be1, W_in2, b_in2, W_out2, b_out2, W_self2, b_self2, g2, be2):
        import jax, jax.numpy as jnp
        import numpy as np
        THRESH = 1e-06
        EPS = 1e-08
        LN_EPS = 1e-05

        def _layer(h, M, W_in, b_in, W_out, b_out, W_self, b_self, gamma, beta):
            A = M / (jnp.sum(M, axis=0, keepdims=True) + EPS)
            mask = A > THRESH
            W = jnp.where(mask, A, 0.0)
            T = h @ W_in + b_in
            weighted_sum = jnp.einsum('ji,jd->id', W, T)
            weight_sum = jnp.sum(W, axis=0)
            has_edge = jnp.any(mask, axis=0)
            agg = jnp.where(has_edge[:, None], weighted_sum / (weight_sum[:, None] + EPS), T)
            agg = agg @ W_out + b_out
            out = agg + (h @ W_self + b_self)
            mu = jnp.mean(out, axis=-1, keepdims=True)
            var = jnp.mean(jnp.square(out - mu), axis=-1, keepdims=True)
            out = (out - mu) * jax.lax.rsqrt(var + LN_EPS) * gamma + beta
            return out
        h = _layer(node_features, mobility_matrix, W_in1, b_in1, W_out1, b_out1, W_self1, b_self1, g1, be1)
        h = jax.nn.relu(h)
        h = _layer(h, mobility_matrix, W_in2, b_in2, W_out2, b_out2, W_self2, b_self2, g2, be2)
        h = jax.nn.relu(h)
        return h

    def _L1_gnn_ref(h, adj, W1, W2, b):
        import jax, jax.numpy as jnp
        import numpy as np
        N = 10000
        D = 128
        F = 128
        K = F // 8
        node = h @ W1
        hw = jnp.einsum('nc,kcf->nkf', h, W2)
        x = jnp.einsum('nk,nkf->nf', node, hw)
        x = adj @ x
        x = x + node @ b
        return jax.nn.relu(x)

    def _L2_gnn_ref(X, S, W1, W2, W3, U1, U2, ln_g, ln_b):
        import jax, jax.numpy as jnp
        import numpy as np
        D_IN = 128
        D_ATTN = 64
        STEPS = 2
        TOP_P = 0.9
        TAU = 1.0
        LN_EPS = 1e-05
        N_NODES = 4096

        def _top_p_attention(X, W1, W2, W3):
            q = X @ W1.T @ W2.T
            k = X @ W3.T
            logits = q @ k.T / TAU
            probs = jax.nn.softmax(logits, axis=-1)
            idx = jnp.argsort(-probs, axis=-1)
            sp = jnp.take_along_axis(probs, idx, axis=-1)
            cs = jnp.cumsum(sp, axis=-1)
            keep_sorted = cs - sp < TOP_P
            rows = jnp.arange(probs.shape[0])[:, None]
            mask = jnp.zeros(probs.shape, dtype=bool).at[rows, idx].set(keep_sorted)
            A = probs * mask
            return A / jnp.maximum(A.sum(-1, keepdims=True), 1e-12)
        N = X.shape[0]
        R = S + jnp.eye(N, dtype=X.dtype)
        R = R / R.sum(-1, keepdims=True)
        Z = jnp.zeros_like(X)
        Xf = X
        Xa = X
        for n in range(STEPS):
            A = _top_p_attention(Xa, W1, W2, W3)
            Xf = R @ Xf
            Xa = A @ Xa
            Z = Z + Xf @ U1[n].T + Xa @ U2[n].T
        h = X + Z
        mu = h.mean(-1, keepdims=True)
        var = jnp.mean((h - mu) ** 2, axis=-1, keepdims=True)
        return (h - mu) / jnp.sqrt(var + LN_EPS) * ln_g + ln_b

    def _L3_gnn_ref(z, dist_matrix, W, B):
        import jax, jax.numpy as jnp
        import numpy as np
        N = 4096
        D = 128
        CUTOFF = 1.0
        MU = 1.0
        SIGMA = 0.5

        def sensitivity(r, mu, sigma):
            return jnp.exp(-(1.0 / r - 1.0 / mu) ** 2 / (2.0 * sigma * sigma))
        msg = z @ W + B
        sens = sensitivity(dist_matrix, MU, SIGMA)
        weights = jnp.where(dist_matrix < CUTOFF, sens, 0.0)
        return weights @ msg
    h = jnp.maximum(_layernorm(x, axis=-1), 0.0)
    x = x + _L0_gnn_ref(h, adj, L0_gnn_W_in1, L0_gnn_b_in1, L0_gnn_W_out1, L0_gnn_b_out1, L0_gnn_W_self1, L0_gnn_b_self1, L0_gnn_g1, L0_gnn_be1, L0_gnn_W_in2, L0_gnn_b_in2, L0_gnn_W_out2, L0_gnn_b_out2, L0_gnn_W_self2, L0_gnn_b_self2, L0_gnn_g2, L0_gnn_be2)
    h = jnp.maximum(_layernorm(x, axis=-1), 0.0)
    x = x + _L1_gnn_ref(h, adj, L1_gnn_W1, L1_gnn_W2, L1_gnn_b)
    h = jnp.maximum(_layernorm(x, axis=-1), 0.0)
    x = x + _L2_gnn_ref(h, adj, L2_gnn_W1, L2_gnn_W2, L2_gnn_W3, L2_gnn_U1, L2_gnn_U2, L2_gnn_ln_g, L2_gnn_ln_b)
    h = jnp.maximum(_layernorm(x, axis=-1), 0.0)
    x = x + _L3_gnn_ref(h, adj, L3_gnn_W, L3_gnn_B)
    return x

_drawn_inputs = setup_inputs


def setup_inputs(seed=0):
    import zlib

    import numpy as np

    out = dict(_drawn_inputs(seed))
    spreads = {'L0_gnn_b_in1': (0.0, 0.1),
     'L0_gnn_b_out1': (0.0, 0.1),
     'L0_gnn_b_self1': (0.0, 0.1),
     'L0_gnn_g1': (1.0, 0.2),
     'L0_gnn_be1': (0.0, 0.1),
     'L0_gnn_b_in2': (0.0, 0.1),
     'L0_gnn_b_out2': (0.0, 0.1),
     'L0_gnn_b_self2': (0.0, 0.1),
     'L0_gnn_g2': (1.0, 0.2),
     'L0_gnn_be2': (0.0, 0.1),
     'L2_gnn_ln_g': (1.0, 0.2),
     'L2_gnn_ln_b': (0.0, 0.1),
     'L3_gnn_B': (0.0, 0.526)}
    factors = {}
    for name, (base, spread) in spreads.items():
        noise = np.random.default_rng([zlib.crc32(name.encode()), seed]).standard_normal(out[name].shape)
        drawn = base * np.exp(spread * noise) if base else spread * noise
        out[name] = jnp.asarray(drawn.astype(out[name].dtype))
    for name, factor in factors.items():
        out[name] = (out[name] * factor).astype(out[name].dtype)
    return out
```

```python
from contextlib import ExitStack

import concourse.bass as bass
from concourse import mybir

F32 = mybir.dt.float32
F16 = mybir.dt.float16
I32 = mybir.dt.int32
ALU = mybir.AluOpType
ACT = mybir.ActivationFunctionType
AX_X = mybir.AxisListType.X

P = 128
N = 2048
NB = N // P
D = 128
H = 256
KM = 16
DA = 64
CH = 512
NCH = N // CH
GRP = 4
NG = NB // GRP
STEPS = 2
EVALS = 8
HALVINGS = 40
WIDE = 256

THRESH, EPS, LN_EPS, TOP_P, SUM_MIN = 1e-6, 1e-8, 1e-5, 0.9, 1e-12
M_SCALE = 1024.0
V_SCALE = 64.0
UNSCALE = 1.0 / (M_SCALE * V_SCALE)
R_MIN = 1e-15
ONE_BITS = float(0x3F800000)


def gnn_kernel(nc, t, out):
    with ExitStack() as ctx:
        def sb(name, shape, dt=F32):
            return ctx.enter_context(nc.sbuf_tensor(name, shape, dt))

        big = sb("matrix_parts", [P, 2, NB, N], F16)
        arena = sb("arena", [P, 3 * N])
        s1 = sb("s1", [P, NB * H + 128])
        pa = sb("pa", [P, NB, D])
        pb = sb("pb", [P, NB, D])
        zb = sb("zb", [P, NB, D])
        xb = sb("residual", [P, NB, D])
        wbuf = sb("wbuf", [P, 4 * H])
        ps = ctx.enter_context(nc.psum_tensor("ps", [P, 8 * CH], F32))
        ident = sb("ident", [P, P])
        ones16 = sb("ones16", [P, P], F16)
        lnsum, lnvar, lnstd, lninv = (sb(n, [P, NB]) for n in ("lnsum", "lnvar", "lnstd", "lninv"))
        colsum, wsum, inv_w, no_edge, bias_w = (sb(n, [P, NB]) for n in ("colsum", "wsum", "inv_w", "no_edge", "bias_w"))
        minus1 = sb("minus1", [P, 1])

        def flat(a):
            return a[:, :, :].rearrange("p b c -> p (b c)")

        def blocks(a, n=NB):
            return a.rearrange("p (b c) -> p b c", b=n)

        def over(col, w):
            return col.unsqueeze(2).to_broadcast([P, NB, w])

        def along(row, w):
            return row.unsqueeze(1).to_broadcast([P, NB, w])

        raw = [arena[:, s * N:(s + 1) * N] for s in range(2)]
        tail = arena[:, 2 * N:3 * N]
        pair = s1[:, 0:NB * 130].bitcast(F16).rearrange("p (a b c) -> p a b c", a=2, b=NB)
        mask16 = s1[:, NB * 130:NB * 130 + N // 2].bitcast(F16)
        wide = blocks(ps[:, :])
        low4, high4 = blocks(ps[:, 0:N]), blocks(ps[:, N:2 * N])

        hid = blocks(s1[:, 0:NB * H])
        hidT = arena[:, 0:2 * N].rearrange("p (a n) -> p a n", a=2)
        g1, be1, bw1, bo1, bs1 = (tail[:, i * H:(i + 1) * H] for i in range(5))
        g2, be2, bo2, bs2, wout2, bin2_rep = (tail[:, 5 * H + i * D:5 * H + (i + 1) * D] for i in range(6))
        wa1, wself1 = wbuf[:, 0:H], wbuf[:, H:2 * H]
        w2cat = wbuf[:, 2 * H:4 * H].rearrange("p (a c) -> p a c", a=2)
        wtmp = flat(pb)
        winT1 = wtmp[:, 0:256].rearrange("p (a c) -> p a c", a=2)
        wout1 = wtmp[:, 256:768].rearrange("p (a c) -> p a c", a=2)
        winT2 = wtmp[:, 768:1024].rearrange("p (a c) -> p a c", a=2)
        bin1 = wtmp[:, 1024:1026]
        bin2 = wtmp[:, 1026:1027]
        bin1_rep = wtmp[:, 1152:1408].rearrange("p (a c) -> p a c", a=2)
        w2mix = tail
        w1mix = wbuf[:, 0:KM]
        w1mixT = wbuf[0:KM, 16:16 + D]
        bmix = wbuf[0:KM, 144:144 + D]
        w1b = wbuf[:, 272:272 + D]
        node = wbuf[:, 400:400 + NB * KM].rearrange("p (b k) -> p b k", b=NB)
        w1a = wbuf[0:DA, 0:D]
        w2aT = wbuf[0:DA, 128:192]
        w3aT = wbuf[:, 192:256]
        wq = wbuf[:, 256:320]
        u1T = wbuf[:, 320:576].rearrange("p (s c) -> p s c", s=STEPS)
        u2T = wbuf[:, 576:832].rearrange("p (s c) -> p s c", s=STEPS)
        xfT = arena[:, 0:N]
        xf2 = blocks(arena[:, N:2 * N])
        lng, lnb = tail[:, 0:D], tail[:, D:2 * D]
        qT, kT = s1[0:DA, 0:N], s1[0:DA, N:2 * N]
        att = big[:, :, :, :].rearrange("p a b c -> p (a b c)").bitcast(F32)
        ebuf = att[:, 0:2 * GRP * N].rearrange("p (g u n) -> p g u n", g=2, u=GRP)
        atT = att[:, 2 * GRP * N:(2 * GRP + 2) * N].rearrange("p (s n) -> p s n", s=2)
        junk = [att[:, (2 * GRP + 2 + i) * N:(2 * GRP + 3 + i) * N] for i in range(3)]
        unread = [att[:, (2 * GRP + 2) * N + u * N // 2:(2 * GRP + 2) * N + (u + 1) * N // 2].bitcast(F16)
                  for u in range(GRP)]
        small_at = [(2 * GRP + 5) * N]

        def small(*shape, dt=F32):
            n = 1
            for k in shape:
                n *= k
            at = small_at[0]
            small_at[0] += (n + 7) // 8 * 8
            v = att[:, at:at + n]
            if dt != F32:
                v = v.bitcast(dt)
            if len(shape) == 2:
                v = v.rearrange("p (a b) -> p a b", a=shape[0])
            if len(shape) == 3:
                v = v.rearrange("p (a b c) -> p a b c", a=shape[0], b=shape[1])
            return v

        negmax, zsum, asum = small(2, GRP), small(2, GRP), small(2, GRP)
        target = small(GRP)
        bound = small(2, 2, GRP)
        cand = small(2, GRP)
        cand_i = small(GRP, dt=I32)
        cand_f = cand_i.bitcast(F32)
        mass = small(GRP)
        above, below = small(2, GRP), small(2, GRP)
        width = small(2, GRP)
        frac, t1, t2, t3 = small(GRP), small(GRP), small(GRP), small(GRP)
        top8, csum, last, prod8 = (small(GRP, 8) for _ in range(4))
        kept = small(GRP, 9)
        cut = small(GRP)
        ones8 = small(8)
        flags, flagT = small(32), small(32)
        quad = small(4)
        flag_i = small(8, dt=I32)
        gl, gh, gm, gmass, gq = (small(1) for _ in range(5))
        g_up, g_dn = small(1), small(1)

        made = {}

        def sg(name):
            if name not in made:
                made[name] = ctx.enter_context(nc.semaphore(name))
            return made[name]

        block = ctx.enter_context(nc.Block())

        @block.sync
        def _(sp):
            def load(dst, src, name):
                sp.dma_start(dst, src).then_inc(sg(name), 16)

            def rows(ap):
                return ap.rearrange("(b p) d -> p b d", p=P)

            def stream(src, turn):
                for s in range(2):
                    if turn:
                        sp.wait_ge(sg(f"raw_free{s}"), NB // 2 * turn)
                    load(raw[s], src[s * P:(s + 1) * P, :], f"raw_in{s}")
                with sp.Fori(1, NB // 2) as i:
                    for s in range(2):
                        sp.wait_ge(sg(f"raw_free{s}"), i + NB // 2 * turn)
                        load(raw[s], src[bass.ds(i * (2 * P) + s * P, P), :], f"raw_in{s}")

            load(xb[:, :, :], rows(t["x"]), "x_in")
            load(winT1, t["W_inT1"].rearrange("(a p) d -> p a d", p=P), "w0_in")
            load(wout1, t["W_out1"].rearrange("(a p) d -> p a d", p=P), "w0_in")
            load(winT2, t["W_inT2"].rearrange("p (a d) -> p a d", a=2), "w0_in")
            load(bin1, t["b_in1"], "w0_in")
            load(bin2, t["b_in2"], "w0_in")
            load(wself1, t["W_self1"], "w0_in")
            load(w2cat[:, :, D:H], t["W_self2"].rearrange("(a p) d -> p a d", p=P), "w0_in")
            stream(t["adj"], 0)
            stream(t["adj"], 1)
            sp.wait_ge(sg("masked"), 1)
            for dst, n in ((g1, "g1"), (be1, "be1"), (bo1, "b_out1"), (bs1, "b_self1"),
                           (g2, "g2"), (be2, "be2"), (bo2, "b_out2"), (bs2, "b_self2")):
                load(dst, t[n].partition_broadcast(P), "vec0_in")
            load(wout2, t["W_out2"], "vec0_in")
            sp.wait_ge(sg("lin2"), 1)
            load(w1mix, t["W1"], "w1_in")
            load(w1mixT, t["W1T"], "w1_in")
            load(bmix, t["b"], "w1_in")
            stream(t["adjT"], 2)
            sp.wait_ge(sg("x1"), 1)
            load(w2mix, t["W2"], "w2_in")
            sp.wait_ge(sg("x2"), 1)
            load(w1a, t["L2_W1"], "w3_in")
            load(w2aT, t["L2_W2T"], "w3_in")
            load(w3aT, t["L2_W3T"], "w3_in")
            load(u1T, t["U1T"].rearrange("s p c -> p s c"), "w3_in")
            load(u2T, t["U2T"].rearrange("s p c -> p s c"), "w3_in")
            load(lng, t["ln_g"].partition_broadcast(P), "w3_in")
            load(lnb, t["ln_b"].partition_broadcast(P), "w3_in")
            sp.wait_ge(sg("x3"), 1)
            load(wbuf[:, 0:D], t["L3_W"], "w4_in")
            load(wbuf[:, D:2 * D], t["L3_B"].partition_broadcast(P), "w4_in")
            stream(t["adjT"], 3)
            sp.wait_ge(sg("x4"), 1)
            load(rows(out), zb[:, :, :], "out_done")
            sp.wait_ge(sg("out_done"), 16)

        @block.gpsimd
        def _(pool):
            nc.gpsimd.memset(ident[:, :], 0.0).then_inc(sg("zeroed"), 1)
            pool.wait_ge(sg("zeroed"), 1)
            nc.gpsimd.affine_select(out=ident[:, :], in_=ident[:, :], compare_op=ALU.not_equal, fill=1.0,
                                    base=0, pattern=[[-1, P]], channel_multiplier=1).then_inc(sg("consts"), 1)
            nc.gpsimd.memset(ones16[:, :], 1.0).then_inc(sg("consts"), 1)
            nc.gpsimd.memset(minus1[:, :], -1.0).then_inc(sg("consts"), 1)

        @block.scalar
        def _(act):
            def root(name):
                act.wait_ge(sg(name + "_var"), 1)
                nc.scalar.activation(lnstd[:, :], lnvar[:, :], ACT.Sqrt).then_inc(sg(name + "_std"), 1)

            def copy(dst, src, name, count=1):
                act.wait_ge(sg(name), count)
                nc.scalar.activation(dst, src, ACT.Copy).then_inc(sg(name + "_out"), 1)

            def split_high(turn, done):
                with act.Fori(0, NB // 2) as i:
                    for s in range(2):
                        act.wait_ge(sg(f"raw_in{s}"), i * 16 + 16 * (NB // 2 * turn + 1))
                        nc.scalar.activation(big[:, 0, i * 2 + s, :], raw[s], ACT.Copy,
                                             scale=M_SCALE).then_inc(sg(done), 1)

            root("ln0")
            split_high(0, "high_adj")
            act.wait_ge(sg("wprod"), 1)
            act.wait_ge(sg("masked"), 1)
            nc.scalar.activation(wa1, ps[:, 0:H], ACT.Copy).then_inc(sg("wprod_out"), 1)
            nc.scalar.activation(w2cat[:, :, 0:D], ps[:, CH:CH + H].rearrange("p (a c) -> p a c", a=2),
                                 ACT.Copy).then_inc(sg("wprod_out"), 1)
            nc.scalar.activation(bw1, ps[:, 2 * CH:2 * CH + H], ACT.Copy).then_inc(sg("wprod_out"), 1)
            copy(arena[:, 0:N], ps[:, 0:N], "uT")
            copy(flat(pb), ps[:, N:2 * N], "h0T")
            root("ln1")
            for a in range(2):
                copy(hidT[:, a, :], ps[:, a * N:(a + 1) * N], "hidT", a + 1)
            root("ln2")
            root("ln3")
            act.wait_ge(sg("prod2"), 1)
            split_high(2, "high_adjT")
            copy(flat(pb), ps[:, 0:N], "h1T")
            copy(w1b, ps[:, N:N + D], "w1b")
            copy(node, ps[:, N + CH:N + CH + NB * KM].rearrange("p (b k) -> p b k", b=NB), "node")
            act.wait_ge(sg("y_pair"), 1)
            copy(flat(zb), ps[:, 0:N], "nodeb")
            root("ln4")
            copy(xfT, ps[:, 0:N], "xf1T")
            act.wait_ge(sg("z_xf1"), 1)
            copy(xfT, ps[:, 0:N], "xf2T")
            copy(wq, ps[:, 0:DA], "wq")
            for st in range(STEPS):
                xT = (pb, pa)[st]
                copy(flat(xT), ps[:, 0:N], "xaT", st + 1)
                copy(qT, ps[0:DA, 0:N], "qT", st + 1)
                copy(kT, ps[0:DA, N:2 * N], "kT", st + 1)

                def exps(g, u):
                    n = st * NB + g * GRP + u
                    act.wait_ge(sg("rowmax"), n + 1)
                    if g >= 2:
                        act.wait_ge(sg("a_turned"), n - 2 * GRP + 1)
                    nc.scalar.activation(ebuf[:, g % 2, u, :], ps[:, 0:N], ACT.Exp, bias=negmax[:, g % 2, u:u + 1],
                                         accum_out=zsum[:, g % 2, u:u + 1]).then_inc(sg("e_ready"), 1)

                def turned(g, u):
                    n = st * NB + g * GRP + u
                    act.wait_ge(sg("a_turned"), n + 1)
                    if n >= 2:
                        act.wait_ge(sg("ax"), n - 1)
                    nc.scalar.activation(atT[:, n % 2, :], ps[:, N:2 * N], ACT.Copy).then_inc(sg("at_out"), 1)

                def mixed(g, u):
                    n = st * NB + g * GRP + u
                    act.wait_ge(sg("ax"), n + 1)
                    nc.scalar.activation(xT[:, g * GRP + u, :], ps[:, N:N + D], ACT.Copy,
                                         scale=asum[:, g % 2, u:u + 1]).then_inc(sg("xa_out"), 1)

                if st:
                    act.wait_ge(sg("z_xa1"), 1)
                for u in range(GRP):
                    exps(0, u)
                for g in range(NG + 1):
                    for u in range(GRP):
                        if g >= 1:
                            turned(g - 1, u)
                        if g + 1 < NG:
                            exps(g + 1, u)
                        if g >= 1:
                            mixed(g - 1, u)
            copy(flat(pb), ps[:, 0:N], "xaT", 3)
            root("ln5")
            root("ln6")
            copy(flat(pb), ps[:, 0:N], "h3T")
            with act.Fori(0, NB // 2) as i:
                for s in range(2):
                    act.wait_ge(sg("inverse"), i * 2 + s + 1)
                    nc.scalar.activation(tail, tail, ACT.Square, bias=minus1[:, 0:1]).then_inc(sg("sens_sq"), 1)
                    act.wait_ge(sg("sens_sq"), i * 2 + s + 1)
                    nc.scalar.activation(tail, tail, ACT.Exp, scale=-2.0).then_inc(sg("sens"), 1)
                    act.wait_ge(sg("weights"), i * 2 + s + 1)
                    nc.scalar.activation(big[:, 0, i * 2 + s, :], tail, ACT.Copy,
                                         scale=M_SCALE).then_inc(sg("high_w"), 1)

        @block.tensor
        def _(pe):
            def turn(src, col0, name):
                for b in range(NB):
                    mm = nc.tensor.transpose(ps[:, col0 + b * P:col0 + (b + 1) * P], src[:, b, :], ident[:, :])
                mm.then_inc(sg(name), 1)

            def linear(srcT, w, col0, name):
                for b in range(NB):
                    mm = nc.tensor.matmul(ps[:, col0 + b * P:col0 + (b + 1) * P], flat(srcT)[:, b * P:(b + 1) * P], w,
                                          start=True, stop=True)
                mm.then_inc(sg(name), 1)

            def tick(name):
                pe.wait_ge(sg(name + "_blk"), NB)
                nc.tensor.matmul(ps[0:1, 8 * CH - 1:8 * CH], ones16[0:1, 0:1], ones16[0:1, 0:1],
                                 start=True, stop=True).then_inc(sg(name), 1)

            def product(w, name):
                with pe.Fori(0, NB) as i:
                    for j in range(NB):
                        for n, (a, v) in enumerate(((0, 0), (0, 1), (1, 0))):
                            mm = nc.tensor.matmul(ps[:, bass.ds(i * WIDE, w)],
                                                  big[:, a, j, bass.ts(i, P)], pair[:, v, j, 0:w],
                                                  start=(j == 0 and n == 0), stop=(j == NB - 1 and n == 2))
                    mm.then_inc(sg(name + "_blk"), 1)
                tick(name)

            pe.wait_ge(sg("consts"), 3)
            with pe.Fori(0, NB) as i:
                pe.wait_ge(sg("low_adj"), i + 1)
                for c in range(NCH):
                    for a in range(2):
                        mm = nc.tensor.matmul(ps[:, (c + 4 * a) * CH:(c + 4 * a + 1) * CH], ones16[:, :],
                                              big[:, a, i, c * CH:(c + 1) * CH], start=False, stop=False,
                                              skip_group_check=True)
                mm.then_inc(sg("colsum_mm"), 1)
            pe.wait_ge(sg("w0_in"), 16 * 7)
            pe.wait_ge(sg("vec0_in"), 16 * 9)
            pe.wait_ge(sg("bin_rep"), 1)
            pe.wait_ge(sg("thresholds"), 1)
            for a in range(2):
                nc.tensor.matmul(ps[:, 0:H], winT1[:, a, :], wout1[:, a, :], start=(a == 0), stop=(a == 1))
            for a in range(2):
                nc.tensor.matmul(ps[:, CH + a * D:CH + (a + 1) * D], winT2[:, a, :], wout2, start=True, stop=True)
            for a in range(2):
                mm = nc.tensor.matmul(ps[:, 2 * CH:2 * CH + H], bin1_rep[:, a, :], wout1[:, a, :],
                                      start=(a == 0), stop=(a == 1))
            mm.then_inc(sg("wprod"), 1)
            pe.wait_ge(sg("wprod_out"), 3)
            pe.wait_ge(sg("masked"), 1)
            pe.wait_ge(sg("h0_pair"), 1)
            product(D + 1, "prod1")
            pe.wait_ge(sg("u"), 1)
            turn(zb, 0, "uT")
            turn(pa, N, "h0T")
            pe.wait_ge(sg("uT_out"), 1)
            pe.wait_ge(sg("h0T_out"), 1)
            for b in range(NB):
                o = ps[:, b * H:(b + 1) * H]
                nc.tensor.matmul(o, arena[:, b * P:(b + 1) * P], wa1, start=True, stop=False)
                mm = nc.tensor.matmul(o, flat(pb)[:, b * P:(b + 1) * P], wself1, start=False, stop=True)
            mm.then_inc(sg("lin1"), 1)
            pe.wait_ge(sg("hid"), 1)
            for a in range(2):
                for b in range(NB):
                    mm = nc.tensor.transpose(ps[:, a * N + b * P:a * N + (b + 1) * P], hid[:, b, a * P:(a + 1) * P],
                                             ident[:, :])
                mm.then_inc(sg("hidT"), 1)
            pe.wait_ge(sg("hidT_out"), 2)
            for b in range(NB):
                o = ps[:, b * H:(b + 1) * H]
                nc.tensor.matmul(o, hidT[:, 0, b * P:(b + 1) * P], w2cat[:, 0, :], start=True, stop=False)
                nc.tensor.matmul(ps[:, b * H:b * H + D], bin2_rep, wout2, start=False, stop=False)
                mm = nc.tensor.matmul(o, hidT[:, 1, b * P:(b + 1) * P], w2cat[:, 1, :], start=False, stop=True)
            mm.then_inc(sg("lin2"), 1)
            pe.wait_ge(sg("p_pair"), 1)
            product(D, "prod2")
            pe.wait_ge(sg("h1"), 1)
            turn(pa, 0, "h1T")
            pe.wait_ge(sg("w1_in"), 16 * 3)
            nc.tensor.matmul(ps[:, N:N + D], w1mixT, bmix, start=True, stop=True).then_inc(sg("w1b"), 1)
            pe.wait_ge(sg("h1T_out"), 1)
            for b in range(NB):
                mm = nc.tensor.matmul(ps[:, N + CH + b * KM:N + CH + (b + 1) * KM], flat(pb)[:, b * P:(b + 1) * P],
                                      w1mix, start=True, stop=True)
            mm.then_inc(sg("node"), 1)
            pe.wait_ge(sg("w1b_out"), 1)
            pe.wait_ge(sg("node_out"), 1)
            pe.wait_ge(sg("w2_in"), 16)
            for b in range(NB):
                if b >= 2:
                    pe.wait_ge(sg("mix_used"), b - 1)
                for c in range(NCH):
                    o = (b % 2 * NCH + c) * CH
                    mm = nc.tensor.matmul(ps[:, o:o + CH], flat(pb)[:, b * P:(b + 1) * P],
                                          w2mix[:, c * CH:(c + 1) * CH], start=True, stop=True)
                mm.then_inc(sg("mix_mm"), 1)
            pe.wait_ge(sg("mix_used"), NB)
            linear(pb, w1b, 0, "nodeb")
            pe.wait_ge(sg("nodeb_out"), 1)
            pe.wait_ge(sg("y_pair"), 1)
            pe.wait_ge(sg("adjT_split"), 1)
            product(D, "prod3")
            pe.wait_ge(sg("h2_pair"), 1)
            product(D + 1, "prod4")
            pe.wait_ge(sg("xf1"), 1)
            turn(pb, 0, "xf1T")
            pe.wait_ge(sg("xf1T_out"), 1)
            pe.wait_ge(sg("w3_in"), 16 * 7)
            for b in range(NB):
                mm = nc.tensor.matmul(ps[:, N + b * P:N + (b + 1) * P], xfT[:, b * P:(b + 1) * P], u1T[:, 0, :],
                                      start=True, stop=True)
            mm.then_inc(sg("zxf1"), 1)
            pe.wait_ge(sg("z_xf1"), 1)
            pe.wait_ge(sg("xf1_pair"), 1)
            product(D, "prod5")
            pe.wait_ge(sg("xf2"), 1)
            turn(xf2, 0, "xf2T")
            pe.wait_ge(sg("xf2T_out"), 1)
            for b in range(NB):
                mm = nc.tensor.matmul(ps[:, N + b * P:N + (b + 1) * P], xfT[:, b * P:(b + 1) * P], u1T[:, 1, :],
                                      start=True, stop=True)
            mm.then_inc(sg("zxf2"), 1)
            nc.tensor.matmul(ps[:, 0:DA], w1a, w2aT, start=True, stop=True).then_inc(sg("wq"), 1)
            pe.wait_ge(sg("wq_out"), 1)
            pe.wait_ge(sg("z_xf2"), 1)
            for st in range(STEPS):
                xa, xT = ((pa, pb), (pb, pa))[st]
                turn(xa, 0, "xaT")
                pe.wait_ge(sg("xaT_out"), st + 1)
                for c in range(NCH):
                    mm = nc.tensor.matmul(ps[0:DA, c * CH:(c + 1) * CH], wq, flat(xT)[:, c * CH:(c + 1) * CH],
                                          start=True, stop=True)
                mm.then_inc(sg("qT"), 1)
                for c in range(NCH):
                    mm = nc.tensor.matmul(ps[0:DA, N + c * CH:N + (c + 1) * CH], w3aT, flat(xT)[:, c * CH:(c + 1) * CH],
                                          start=True, stop=True)
                mm.then_inc(sg("kT"), 1)
                pe.wait_ge(sg("qT_out"), st + 1)
                pe.wait_ge(sg("kT_out"), st + 1)
                if st:
                    linear(xT, u2T[:, 0, :], N, "zxa1")
                    pe.wait_ge(sg("z_xa1"), 1)

                def logits(g, u):
                    n = st * NB + g * GRP + u
                    if n:
                        pe.wait_ge(sg("e_ready"), n)
                    for c in range(NCH):
                        mm = nc.tensor.matmul(ps[:, c * CH:(c + 1) * CH], qT[:, (g * GRP + u) * P:(g * GRP + u + 1) * P],
                                              kT[:, c * CH:(c + 1) * CH], start=True, stop=True)
                    mm.then_inc(sg("logits"), 1)

                def turn_a(g, u):
                    n = st * NB + g * GRP + u
                    if u == 0:
                        pe.wait_ge(sg("a_ready"), st * NG + g + 1)
                    if n:
                        pe.wait_ge(sg("xa_out"), n)
                    for j in range(NB):
                        mm = nc.tensor.transpose(ps[:, N + j * P:N + (j + 1) * P],
                                                 ebuf[:, g % 2, u, j * P:(j + 1) * P], ident[:, :])
                    mm.then_inc(sg("a_turned"), 1)

                def mix_a(g, u):
                    n = st * NB + g * GRP + u
                    pe.wait_ge(sg("at_out"), n + 1)
                    for j in range(NB):
                        mm = nc.tensor.matmul(ps[:, N:N + D], atT[:, n % 2, j * P:(j + 1) * P], xa[:, j, :],
                                              start=(j == 0), stop=(j == NB - 1))
                    mm.then_inc(sg("ax"), 1)

                for u in range(GRP):
                    logits(0, u)
                for g in range(NG + 1):
                    for u in range(GRP):
                        if g >= 1:
                            turn_a(g - 1, u)
                        if g + 1 < NG:
                            logits(g + 1, u)
                        if g >= 1:
                            mix_a(g - 1, u)
                pe.wait_ge(sg("xa_out"), NB * (st + 1))
            turn(pa, 0, "xaT")
            pe.wait_ge(sg("xaT_out"), 3)
            linear(pb, u2T[:, 1, :], N, "zxa2")
            pe.wait_ge(sg("h3"), 1)
            turn(pa, 0, "h3T")
            pe.wait_ge(sg("h3T_out"), 1)
            pe.wait_ge(sg("w4_in"), 16 * 2)
            linear(pb, wbuf[:, 0:D], N, "msg")
            pe.wait_ge(sg("msg_pair"), 1)
            pe.wait_ge(sg("w_split"), 1)
            product(D, "prod6")

        @block.vector
        def _(dve):
            v = nc.vector
            done = [0]

            def step(ins):
                ins.then_inc(sg("dve_step"), 1)
                done[0] += 1
                dve.wait_ge(sg("dve_step"), done[0])

            def tell(ins, name, count=1):
                ins.then_inc(sg(name), 1)
                dve.wait_ge(sg(name), count)

            def layernorm(src, dst, tmp, w, name, gamma=None, beta=None, relu=True):
                step(v.tensor_reduce(lnsum[:, :], src, AX_X, ALU.add))
                step(v.tensor_scalar(lnsum[:, :], lnsum[:, :], 1.0 / w, None, ALU.mult))
                step(v.tensor_tensor(dst, src, over(lnsum[:, :], w), ALU.subtract))
                step(v.tensor_tensor(tmp, dst, dst, ALU.mult))
                step(v.tensor_reduce(lnvar[:, :], tmp, AX_X, ALU.add))
                tell(v.tensor_scalar(lnvar[:, :], lnvar[:, :], 1.0 / w, LN_EPS, ALU.mult, ALU.add), name + "_var")
                dve.wait_ge(sg(name + "_std"), 1)
                step(v.reciprocal(lninv[:, :], lnstd[:, :]))
                step(v.tensor_tensor(dst, dst, over(lninv[:, :], w), ALU.mult))
                if gamma is not None:
                    step(v.tensor_tensor(dst, dst, along(gamma, w), ALU.mult))
                    step(v.tensor_tensor(dst, dst, along(beta, w), ALU.add))
                if relu:
                    step(v.tensor_scalar(dst, dst, 0.0, None, ALU.max))

            def make_pair(src, name, ones=False):
                step(v.tensor_scalar(pair[:, 0, :, 0:D], src, V_SCALE, None, ALU.mult))
                if ones:
                    step(v.memset(pair[:, 0, :, D:D + 1], 1.0))
                    step(v.memset(pair[:, 1, :, D:D + 1], 0.0))
                tell(v.scalar_tensor_tensor(out=pair[:, 1, :, 0:D], in0=src, scalar=V_SCALE, in1=pair[:, 0, :, 0:D],
                                            op0=ALU.mult, op1=ALU.subtract), name)

            def split_low(high, low, base):
                with dve.Fori(0, NB // 2) as i:
                    for s in range(2):
                        dve.wait_ge(sg(high), i * 2 + s + 1)
                        v.scalar_tensor_tensor(out=big[:, 1, i * 2 + s, :], in0=raw[s], scalar=M_SCALE,
                                               in1=big[:, 0, i * 2 + s, :], op0=ALU.mult,
                                               op1=ALU.subtract).then_inc(sg(low), 1)
                        dve.wait_ge(sg(low), i * 2 + s + 1)
                        v.memset(t_free[s][:, :], 0.0).then_inc(sg(f"raw_free{s}"), 1)

            t_free = [sb(f"t_free{s}", [P, 1]) for s in range(2)]

            step(v.memset(ps[:, :], 0.0))
            dve.wait_ge(sg("x_in"), 16)
            layernorm(xb[:, :, :], pa[:, :, :], zb[:, :, :], D, "ln0")
            make_pair(pa[:, :, :], "h0_pair", ones=True)
            split_low("high_adj", "low_adj", 0)
            dve.wait_ge(sg("w0_in"), 16 * 7)
            dve.wait_ge(sg("colsum_mm"), NB)
            step(v.tensor_scalar(tail, ps[:, 0:N], 1.0 / M_SCALE, EPS, ALU.mult, ALU.add))
            step(v.scalar_tensor_tensor(out=tail, in0=ps[:, N:2 * N], scalar=1.0 / M_SCALE, in1=tail,
                                        op0=ALU.mult, op1=ALU.add))
            dve.wait_ge(sg("consts"), 3)
            step(v.tensor_tensor(zb[:, :, :], blocks(tail), along(ident[:, :], D), ALU.mult))
            step(v.tensor_reduce(colsum[:, :], zb[:, :, :], AX_X, ALU.add))
            tell(v.tensor_scalar(tail, tail, THRESH, None, ALU.mult), "thresholds")
            with dve.Fori(0, NB // 2) as i:
                for s in range(2):
                    dve.wait_ge(sg(f"raw_in{s}"), i * 16 + 16 * (NB // 2 + 1))
                    v.tensor_tensor(mask16, raw[s], tail, ALU.is_gt).then_inc(sg(f"raw_free{s}"), 1)
                    dve.wait_ge(sg(f"raw_free{s}"), i + NB // 2 + 1)
                    for a in range(2):
                        m = big[:, a, i * 2 + s, :]
                        v.tensor_tensor(m, m, mask16, ALU.mult).then_inc(sg("mask_mul"), 1)
                    dve.wait_ge(sg("mask_mul"), i * 4 + s * 2 + 2)
            for a in range(2):
                step(v.tensor_scalar(bin1_rep[:, a, :], zb[:, 0, :], 0.0, bin1[:, a:a + 1], ALU.mult, ALU.add))
            tell(v.memset(t_free[0][:, :], 0.0), "masked")
            tell(v.tensor_scalar(bin2_rep, zb[:, 0, :], 0.0, bin2, ALU.mult, ALU.add), "bin_rep")
            dve.wait_ge(sg("prod1"), 1)
            step(v.tensor_scalar(wsum[:, :], wide[:, :, D], 1.0 / M_SCALE, None, ALU.mult))
            step(v.tensor_scalar(no_edge[:, :], wsum[:, :], 0.0, None, ALU.is_le))
            step(v.scalar_tensor_tensor(out=inv_w[:, :], in0=colsum[:, :], scalar=EPS, in1=wsum[:, :],
                                        op0=ALU.mult, op1=ALU.add))
            step(v.reciprocal(inv_w[:, :], inv_w[:, :]))
            step(v.tensor_tensor(bias_w[:, :], wsum[:, :], inv_w[:, :], ALU.mult))
            step(v.tensor_tensor(bias_w[:, :], bias_w[:, :], no_edge[:, :], ALU.add))
            step(v.tensor_scalar(inv_w[:, :], inv_w[:, :], UNSCALE, None, ALU.mult))
            dve.wait_ge(sg("vec0_in"), 16 * 9)
            dve.wait_ge(sg("wprod_out"), 3)
            step(v.tensor_tensor(zb[:, :, :], pa[:, :, :], over(no_edge[:, :], D), ALU.mult))
            step(v.tensor_tensor(pb[:, :, :], wide[:, :, 0:D], over(inv_w[:, :], D), ALU.mult))
            tell(v.tensor_tensor(zb[:, :, :], zb[:, :, :], pb[:, :, :], ALU.add), "u")
            step(v.tensor_tensor(bo1, bo1, bs1, ALU.add))
            step(v.tensor_tensor(bo2, bo2, bs2, ALU.add))
            step(v.tensor_tensor(hid, along(bw1, H), over(bias_w[:, :], H), ALU.mult))
            step(v.tensor_tensor(hid, hid, along(bo1, H), ALU.add))
            dve.wait_ge(sg("lin1"), 1)
            step(v.tensor_tensor(hid, hid, wide, ALU.add))
            layernorm(hid, hid, blocks(arena[:, 0:2 * N]), H, "ln1", g1, be1)
            tell(v.memset(t_free[0][:, :], 0.0), "hid")
            dve.wait_ge(sg("lin2"), 1)
            step(v.tensor_copy(pb[:, :, :], wide[:, :, 0:D]))
            step(v.tensor_tensor(zb[:, :, :], wide[:, :, D:H], along(bo2, D), ALU.add))
            make_pair(pb[:, :, :], "p_pair")
            step(v.tensor_tensor(pb[:, :, :], pb[:, :, :], over(no_edge[:, :], D), ALU.mult))
            step(v.tensor_tensor(zb[:, :, :], zb[:, :, :], pb[:, :, :], ALU.add))
            dve.wait_ge(sg("prod2"), 1)
            step(v.tensor_tensor(pa[:, :, :], wide[:, :, 0:D], over(inv_w[:, :], D), ALU.mult))
            step(v.tensor_tensor(pa[:, :, :], pa[:, :, :], zb[:, :, :], ALU.add))
            layernorm(pa[:, :, :], pa[:, :, :], zb[:, :, :], D, "ln2", g2, be2)
            tell(v.tensor_tensor(xb[:, :, :], xb[:, :, :], pa[:, :, :], ALU.add), "x1")
            layernorm(xb[:, :, :], pa[:, :, :], zb[:, :, :], D, "ln3")
            tell(v.memset(t_free[0][:, :], 0.0), "h1")
            split_low("high_adjT", "low_adjT", 2)
            tell(v.memset(t_free[0][:, :], 0.0), "adjT_split")
            dve.wait_ge(sg("node_out"), 1)
            with dve.Fori(0, NB // 2) as i:
                for s in range(2):
                    b = i * 2 + s
                    dve.wait_ge(sg("mix_mm"), b + 1)
                    for k in range(KM):
                        o = s * N + k * D
                        src, w = ps[:, o:o + D], node[:, b, k:k + 1]
                        if k == 0:
                            ins = v.tensor_scalar(zb[:, b, :], src, w, None, ALU.mult)
                        else:
                            ins = v.scalar_tensor_tensor(out=zb[:, b, :], in0=src, scalar=w, in1=zb[:, b, :],
                                                         op0=ALU.mult, op1=ALU.add)
                        ins.then_inc(sg("mix_add"), 1)
                        dve.wait_ge(sg("mix_add"), b * KM + k + 1)
                    v.memset(t_free[0][:, :], 0.0).then_inc(sg("mix_used"), 1)
            make_pair(zb[:, :, :], "y_pair")
            dve.wait_ge(sg("nodeb_out"), 1)
            dve.wait_ge(sg("prod3"), 1)
            step(v.scalar_tensor_tensor(out=pa[:, :, :], in0=wide[:, :, 0:D], scalar=UNSCALE, in1=zb[:, :, :],
                                        op0=ALU.mult, op1=ALU.add))
            tell(v.scalar_tensor_tensor(out=xb[:, :, :], in0=pa[:, :, :], scalar=0.0, in1=xb[:, :, :],
                                        op0=ALU.max, op1=ALU.add), "x2")
            layernorm(xb[:, :, :], pa[:, :, :], zb[:, :, :], D, "ln4")
            step(v.tensor_copy(zb[:, :, :], pa[:, :, :]))
            make_pair(pa[:, :, :], "h2_pair", ones=True)
            dve.wait_ge(sg("prod4"), 1)
            step(v.tensor_scalar(wsum[:, :], wide[:, :, D], 1.0 / M_SCALE, 1.0, ALU.mult, ALU.add))
            step(v.reciprocal(wsum[:, :], wsum[:, :]))
            step(v.scalar_tensor_tensor(out=pb[:, :, :], in0=wide[:, :, 0:D], scalar=UNSCALE, in1=pa[:, :, :],
                                        op0=ALU.mult, op1=ALU.add))
            tell(v.tensor_tensor(pb[:, :, :], pb[:, :, :], over(wsum[:, :], D), ALU.mult), "xf1")
            make_pair(pb[:, :, :], "xf1_pair")
            dve.wait_ge(sg("zxf1"), 1)
            tell(v.tensor_tensor(zb[:, :, :], zb[:, :, :], high4, ALU.add), "z_xf1")
            dve.wait_ge(sg("prod5"), 1)
            step(v.scalar_tensor_tensor(out=xf2, in0=wide[:, :, 0:D], scalar=UNSCALE, in1=pb[:, :, :],
                                        op0=ALU.mult, op1=ALU.add))
            tell(v.tensor_tensor(xf2, xf2, over(wsum[:, :], D), ALU.mult), "xf2")
            dve.wait_ge(sg("zxf2"), 1)
            tell(v.tensor_tensor(zb[:, :, :], zb[:, :, :], high4, ALU.add), "z_xf2")
            step(v.memset(ones8, 1.0))
            step(v.memset(kept[:, :, 8:9], 0.0))
            step(v.memset(flags, 0.0))

            def bc2(a):
                return a.unsqueeze(1).to_broadcast([P, 2, GRP])

            loops = [0]

            def row_max(st, g, u, n_const, k):
                dve.wait_ge(sg("logits"), k + (n_const + 1))
                v.tensor_reduce(negmax[:, g % 2, bass.ds(k, 1)] if u is None else negmax[:, g % 2, u:u + 1],
                                ps[:, 0:N], AX_X, ALU.max, negate=True).then_inc(sg("rowmax"), 1)

            def evaluations(g, count, produce):
                base = loops[0]
                per = 4
                with dve.Fori(0, count) as k:
                    for u in range(GRP):
                        e = ebuf[:, g % 2, u, :]
                        ins = v.scalar_tensor_tensor(out=unread[u], in0=e, scalar=cand_f[:, u:u + 1], in1=e,
                                                     op0=ALU.is_gt, op1=ALU.mult, accum_out=mass[:, u:u + 1])
                    dve.drain()
                    v.tensor_tensor(cand[:, 1, :], mass, target, ALU.subtract)
                    v.tensor_scalar(bound[:, :, 1, :], bound[:, :, 1, :], 0.6, None, ALU.mult)
                    dve.drain()
                    v.tensor_scalar(above, bc2(cand[:, 1, :]), 0.0, None, ALU.is_ge)
                    v.tensor_scalar(below, bc2(cand[:, 1, :]), 0.0, None, ALU.is_lt)
                    dve.drain()
                    v.copy_predicated(bound[:, 0, :, :], above.bitcast(I32), cand)
                    v.copy_predicated(bound[:, 1, :, :], below.bitcast(I32), cand)
                    dve.drain()
                    v.tensor_tensor(width, bound[:, 1, :, :], bound[:, 0, :, :], ALU.subtract)
                    v.scalar_tensor_tensor(out=frac, in0=cand_f, scalar=-4.0, in1=bound[:, 0, 1, :],
                                           op0=ALU.mult, op1=ALU.subtract)
                    dve.drain()
                    v.reciprocal(t1, width[:, 1, :])
                    dve.drain()
                    v.tensor_tensor(frac, frac, t1, ALU.mult)
                    dve.drain()
                    v.tensor_scalar(frac, frac, 0.98, 0.02, ALU.min, ALU.max)
                    dve.drain()
                    v.tensor_tensor(frac, frac, width[:, 0, :], ALU.mult)
                    dve.drain()
                    v.tensor_tensor(cand[:, 0, :], frac, bound[:, 0, 0, :], ALU.add)
                    dve.drain()
                    v.tensor_copy(cand_i, cand[:, 0, :])
                    if produce is not None:
                        row_max(None, g + 1, None, produce, k)
                    dve.drain()
                loops[0] += count * per

            def general(g):
                with dve.Fori(0, GRP) as u:
                    e = ebuf[:, g % 2, u, :]
                    tg, zs = target[:, bass.ds(u, 1)], zsum[:, g % 2, bass.ds(u, 1)]
                    v.tensor_scalar(gl, zs, 0.0999 / N, None, ALU.mult)
                    v.memset(gh, 1.0)
                    v.memset(gmass, 0.0)
                    dve.drain()
                    with dve.Fori(0, HALVINGS) as _:
                        v.tensor_scalar(gm, gl, gh[:, 0:1], 0.5, ALU.add, ALU.mult)
                        dve.drain()
                        v.scalar_tensor_tensor(out=junk[0], in0=e, scalar=gm[:, 0:1], in1=e, op0=ALU.is_gt, op1=ALU.mult,
                                               accum_out=gq)
                        dve.drain()
                        v.tensor_tensor(g_up, gq, tg, ALU.is_ge)
                        v.tensor_tensor(g_dn, gq, tg, ALU.is_lt)
                        dve.drain()
                        v.copy_predicated(gl, g_up.bitcast(I32), gm)
                        v.copy_predicated(gh, g_dn.bitcast(I32), gm)
                        v.copy_predicated(gmass, g_dn.bitcast(I32), gq)
                        dve.drain()
                    v.tensor_tensor(gq, tg, gmass, ALU.subtract)
                    v.reciprocal(gm, gh)
                    v.tensor_scalar(junk[0], e, gh[:, 0:1], None, ALU.is_equal)
                    v.memset(junk[1], 1.0)
                    dve.drain()
                    v.tensor_scalar(gq, gq, gm[:, 0:1], 1.0, ALU.mult, ALU.add)
                    v.tensor_tensor_scan(junk[2], junk[1], junk[0], 0.0, ALU.mult, ALU.add)
                    dve.drain()
                    v.scalar_tensor_tensor(out=junk[0], in0=junk[2], scalar=gq[:, 0:1], in1=junk[0],
                                           op0=ALU.is_lt, op1=ALU.mult)
                    dve.drain()
                    v.scalar_tensor_tensor(out=junk[0], in0=e, scalar=gh[:, 0:1], in1=junk[0],
                                           op0=ALU.is_gt, op1=ALU.add)
                    dve.drain()
                    v.scalar_tensor_tensor(out=e, in0=e, scalar=1.0, in1=junk[0], op0=ALU.mult, op1=ALU.mult,
                                           accum_out=asum[:, g % 2, bass.ds(u, 1)])
                    dve.drain()

            def search(st, g):
                base = st * NB + g * GRP
                dve.wait_ge(sg("e_ready"), base + GRP)
                zs = zsum[:, g % 2, :]
                step(v.tensor_scalar(target, zs, TOP_P, None, ALU.mult))
                step(v.tensor_scalar(t1, zs, 0.0999 / N, None, ALU.mult))
                step(v.tensor_copy(bound[:, 0, 0, :], t1.bitcast(I32)))
                step(v.memset(bound[:, 1, 0, :], ONE_BITS))
                step(v.tensor_tensor(bound[:, 0, 1, :], zs, target, ALU.subtract))
                step(v.tensor_scalar(bound[:, 1, 1, :], target, -1.0, None, ALU.mult))
                step(v.tensor_scalar(cand[:, 0, :], bound[:, 0, 0, :], 0.75, 0.25 * ONE_BITS, ALU.mult, ALU.add))
                step(v.tensor_copy(cand_i, cand[:, 0, :]))
                if g + 1 < NG:
                    evaluations(g, GRP, base + GRP)
                    evaluations(g, EVALS - GRP, None)
                else:
                    evaluations(g, EVALS, None)
                step(v.tensor_copy(cand_i, bound[:, 1, 0, :]))
                for u in range(GRP):
                    e = ebuf[:, g % 2, u, :]
                    step(v.scalar_tensor_tensor(out=junk[u % 2], in0=e, scalar=cand_f[:, u:u + 1], in1=e,
                                                op0=ALU.is_le, op1=ALU.mult, accum_out=mass[:, u:u + 1]))
                    step(v.max(top8[:, u, :], junk[u % 2]))
                step(v.tensor_tensor(t1, zs, mass, ALU.subtract))
                for u in range(GRP):
                    step(v.tensor_tensor_scan(csum[:, u, :], ones8, top8[:, u, :], t1[:, u:u + 1], ALU.mult, ALU.add))
                step(v.tensor_tensor(csum, csum, top8, ALU.subtract))
                step(v.tensor_tensor(kept[:, :, 0:8], csum, target.unsqueeze(2).to_broadcast([P, GRP, 8]), ALU.is_lt))
                step(v.tensor_tensor(last, kept[:, :, 0:8], kept[:, :, 1:9], ALU.subtract))
                step(v.tensor_tensor(prod8, last, top8, ALU.mult))
                step(v.tensor_reduce(cut, prod8, AX_X, ALU.add))
                step(v.tensor_tensor(prod8[:, :, 0:7], last[:, :, 0:7], top8[:, :, 1:8], ALU.mult))
                step(v.tensor_reduce(t2, prod8[:, :, 0:7], AX_X, ALU.add))
                step(v.tensor_tensor(t2, t2, cut, ALU.is_equal))
                step(v.tensor_tensor(t2, t2, kept[:, :, 7], ALU.add))
                step(v.tensor_scalar(t3, kept[:, :, 0], -1.0, 1.0, ALU.mult, ALU.add))
                step(v.tensor_tensor(t2, t2, t3, ALU.add))
                step(v.tensor_reduce(flags[:, 0:1], t2, AX_X, ALU.max))
                step(v.transpose(flagT, flags))
                step(v.tensor_reduce(t3[:, 0:1], flagT, AX_X, ALU.max))
                for q in range(4):
                    step(v.tensor_copy(quad[0:1, q:q + 1], t3[32 * q:32 * q + 1, 0:1]))
                step(v.tensor_reduce(flag_i[0:1, 0:1], quad[0:1, :], AX_X, ALU.max))
                if st * NG + g >= 2:
                    dve.wait_ge(sg("xa_out"), base - GRP)
                undecided = dve.value_load(flag_i[0:1, 0:1], min_val=0, max_val=4)
                with dve.If(undecided > 0):
                    general(g)
                with dve.Else():
                    for u in range(GRP):
                        e = ebuf[:, g % 2, u, :]
                        v.scalar_tensor_tensor(out=e, in0=e, scalar=cut[:, u:u + 1], in1=e, op0=ALU.is_ge,
                                               op1=ALU.mult, accum_out=asum[:, g % 2, u:u + 1])
                    dve.drain()
                step(v.tensor_scalar(asum[:, g % 2, :], asum[:, g % 2, :], SUM_MIN, None, ALU.max))
                tell(v.reciprocal(asum[:, g % 2, :], asum[:, g % 2, :]), "a_ready", st * NG + g + 1)

            for st in range(STEPS):
                if st:
                    dve.wait_ge(sg("zxa1"), 1)
                    tell(v.tensor_tensor(zb[:, :, :], zb[:, :, :], high4, ALU.add), "z_xa1")
                for u in range(GRP):
                    row_max(st, 0, u, st * NB + u, 0)
                for g in range(NG):
                    search(st, g)
            dve.wait_ge(sg("zxa2"), 1)
            step(v.tensor_tensor(zb[:, :, :], zb[:, :, :], high4, ALU.add))
            layernorm(zb[:, :, :], zb[:, :, :], pa[:, :, :], D, "ln5", lng, lnb, relu=False)
            tell(v.tensor_tensor(xb[:, :, :], xb[:, :, :], zb[:, :, :], ALU.add), "x3")
            layernorm(xb[:, :, :], pa[:, :, :], zb[:, :, :], D, "ln6")
            tell(v.memset(t_free[0][:, :], 0.0), "h3")
            dve.wait_ge(sg("w4_in"), 16 * 2)
            dve.wait_ge(sg("msg"), 1)
            step(v.tensor_tensor(zb[:, :, :], high4, along(wbuf[:, D:2 * D], D), ALU.add))
            make_pair(zb[:, :, :], "msg_pair")
            with dve.Fori(0, NB // 2) as i:
                for s in range(2):
                    n = i * 2 + s
                    dve.wait_ge(sg(f"raw_in{s}"), i * 16 + 16 * (NB // 2 * 3 + 1))
                    v.tensor_scalar(raw[s], raw[s], R_MIN, None, ALU.max).then_inc(sg("clear"), 1)
                    dve.wait_ge(sg("clear"), n + 1)
                    v.reciprocal(tail, raw[s]).then_inc(sg("inverse"), 1)
                    dve.wait_ge(sg("sens"), n + 1)
                    v.scalar_tensor_tensor(out=tail, in0=raw[s], scalar=1.0, in1=tail, op0=ALU.is_lt,
                                           op1=ALU.mult).then_inc(sg("weights"), 1)
                    dve.wait_ge(sg("high_w"), n + 1)
                    v.scalar_tensor_tensor(out=big[:, 1, n, :], in0=tail, scalar=M_SCALE, in1=big[:, 0, n, :],
                                           op0=ALU.mult, op1=ALU.subtract).then_inc(sg("low_w"), 1)
                    dve.wait_ge(sg("low_w"), n + 1)
                    v.memset(t_free[s][:, :], 0.0).then_inc(sg(f"raw_free{s}"), 1)
            tell(v.memset(t_free[0][:, :], 0.0), "w_split")
            dve.wait_ge(sg("prod6"), 1)
            tell(v.scalar_tensor_tensor(out=zb[:, :, :], in0=wide[:, :, 0:D], scalar=UNSCALE, in1=xb[:, :, :],
                                        op0=ALU.mult, op1=ALU.add), "x4")


def kernel(**inputs):
    import numpy as np
    import concourse.bacc as bacc
    from concourse.bass_utils import run_bass_kernel_spmd as run

    a = {k: np.asarray(v) for k, v in inputs.items()}
    laid = {
        "x": a["x"], "adj": a["adj"], "adjT": a["adj"].T,
        "W_inT1": a["L0_gnn_W_in1"].T, "W_out1": a["L0_gnn_W_out1"], "W_self1": a["L0_gnn_W_self1"],
        "W_inT2": a["L0_gnn_W_in2"].T, "W_out2": a["L0_gnn_W_out2"], "W_self2": a["L0_gnn_W_self2"],
        "W1": a["L1_gnn_W1"], "W1T": a["L1_gnn_W1"].T, "b": a["L1_gnn_b"],
        "W2": a["L1_gnn_W2"].transpose(1, 0, 2).reshape(D, KM * D),
        "L2_W1": a["L2_gnn_W1"], "L2_W2T": a["L2_gnn_W2"].T, "L2_W3T": a["L2_gnn_W3"].T,
        "U1T": a["L2_gnn_U1"].transpose(0, 2, 1), "U2T": a["L2_gnn_U2"].transpose(0, 2, 1),
        "ln_g": a["L2_gnn_ln_g"], "ln_b": a["L2_gnn_ln_b"], "L3_W": a["L3_gnn_W"], "L3_B": a["L3_gnn_B"],
    }
    for s in ("b_in1", "b_out1", "b_self1", "g1", "be1", "b_in2", "b_out2", "b_self2", "g2", "be2"):
        laid[s] = a["L0_gnn_" + s]
    laid["b_in1"], laid["b_in2"] = laid["b_in1"].reshape(2, P).T, laid["b_in2"].reshape(P, 1)
    nc = bacc.Bacc("TRN2", target_bir_lowering=False, num_devices=1)
    laid = {"in_" + k: np.ascontiguousarray(v) for k, v in laid.items()}
    t = {k[3:]: nc.dram_tensor(k, v.shape, F32, kind="ExternalInput").ap() for k, v in laid.items()}
    out = nc.dram_tensor("out", (N, D), F32, kind="ExternalOutput").ap()
    gnn_kernel(nc, t, out)
    return run(nc, [laid], core_ids=[0]).results[0]["out"]
```

```python
from contextlib import ExitStack

import concourse.bass as bass
from concourse import mybir

F32 = mybir.dt.float32
F16 = mybir.dt.float16
I32 = mybir.dt.int32
ALU = mybir.AluOpType
ACT = mybir.ActivationFunctionType
AX_X = mybir.AxisListType.X

P = 128
N = 2048
NB = N // P
D = 128
H = 256
KM = 16
DA = 64
CH = 512
NCH = N // CH
GRP = 4
NG = NB // GRP
STEPS = 2
EVALS = 6
HALVINGS = 40
SEG = 8
WIN = 16
WIDE = 256

THRESH, EPS, LN_EPS, TOP_P, SUM_MIN = 1e-6, 1e-8, 1e-5, 0.9, 1e-12
M_SCALE = 1024.0
V_SCALE = 64.0
UNSCALE = 1.0 / (M_SCALE * V_SCALE)
R_MIN = 1e-15
ONE_BITS = float(0x3F800000)


def gnn_kernel(nc, t, out):
    with ExitStack() as ctx:
        def sb(name, shape, dt=F32):
            return ctx.enter_context(nc.sbuf_tensor(name, shape, dt))

        big = sb("matrix_parts", [P, 2, NB, N], F16)
        arena = sb("arena", [P, 3 * N])
        s1 = sb("s1", [P, NB * H + 128])
        pa = sb("pa", [P, NB, D])
        pb = sb("pb", [P, NB, D])
        zb = sb("zb", [P, NB, D])
        xb = sb("residual", [P, NB, D])
        wbuf = sb("wbuf", [P, 4 * H + 64])
        ps = ctx.enter_context(nc.psum_tensor("ps", [P, 8 * CH], F32))
        ident = sb("ident", [P, P])
        ones16 = sb("ones16", [P, P], F16)
        lnsum, lnvar, lnstd, lninv = (sb(n, [P, NB]) for n in ("lnsum", "lnvar", "lnstd", "lninv"))
        colsum, wsum, inv_w, no_edge, bias_w = (sb(n, [P, NB]) for n in ("colsum", "wsum", "inv_w", "no_edge", "bias_w"))
        minus1, r_min = sb("minus1", [P, 1]), sb("r_min", [P, 1])

        def flat(a):
            return a[:, :, :].rearrange("p b c -> p (b c)")

        def blocks(a, n=NB):
            return a.rearrange("p (b c) -> p b c", b=n)

        def over(col, w):
            return col.unsqueeze(2).to_broadcast([P, NB, w])

        def along(row, w):
            return row.unsqueeze(1).to_broadcast([P, NB, w])

        raw = [arena[:, s * N:(s + 1) * N] for s in range(2)]
        tail = arena[:, 2 * N:3 * N]
        pair = s1[:, 0:NB * 130].bitcast(F16).rearrange("p (a b c) -> p a b c", a=2, b=NB)
        mask16 = s1[:, NB * 130:NB * 130 + N // 2].bitcast(F16)
        wide = blocks(ps[:, :])
        low4, high4 = blocks(ps[:, 0:N]), blocks(ps[:, N:2 * N])

        hid = blocks(s1[:, 0:NB * H])
        hidT = arena[:, 0:2 * N].rearrange("p (a n) -> p a n", a=2)
        g1, be1, bw1, bo1, bs1 = (tail[:, i * H:(i + 1) * H] for i in range(5))
        g2, be2, bo2, bs2, wout2, bin2_rep = (tail[:, 5 * H + i * D:5 * H + (i + 1) * D] for i in range(6))
        wa1, wself1 = wbuf[:, 0:H], wbuf[:, H:2 * H]
        w2cat = wbuf[:, 2 * H:4 * H].rearrange("p (a c) -> p a c", a=2)
        wtmp = flat(pb)
        winT1 = wtmp[:, 0:256].rearrange("p (a c) -> p a c", a=2)
        wout1 = wtmp[:, 256:768].rearrange("p (a c) -> p a c", a=2)
        winT2 = wtmp[:, 768:1024].rearrange("p (a c) -> p a c", a=2)
        bin1 = wtmp[:, 1024:1026]
        bin2 = wtmp[:, 1026:1027]
        bin1_rep = wtmp[:, 1152:1408].rearrange("p (a c) -> p a c", a=2)
        w2mix = tail
        w1mix = wbuf[:, 0:KM]
        w1mixT = wbuf[0:KM, 16:16 + D]
        bmix = wbuf[0:KM, 144:144 + D]
        w1b = wbuf[:, 272:272 + D]
        node = wbuf[:, 400:400 + NB * KM].rearrange("p (b k) -> p b k", b=NB)
        w1a = wbuf[0:DA, 0:D]
        w2aT = wbuf[0:DA, 128:192]
        w3aT = wbuf[:, 192:256]
        wq = wbuf[:, 256:320]
        u1T = wbuf[:, 320:576].rearrange("p (s c) -> p s c", s=STEPS)
        u2T = wbuf[:, 576:832].rearrange("p (s c) -> p s c", s=STEPS)
        xfT = arena[:, 0:N]
        xf2 = blocks(arena[:, N:2 * N])
        lng, lnb = wbuf[:, 832:960], wbuf[:, 960:1088]
        qT, kT = s1[0:DA, 0:N], s1[0:DA, N:2 * N]
        att = big[:, :, :, :].rearrange("p a b c -> p (a b c)").bitcast(F32)
        dist = att.rearrange("p (b n) -> p b n", b=NB)
        sens = [arena[:, s * N:(s + 1) * N] for s in range(3)]
        ratio = s1[:, 0:N]
        ebuf = att[:, 0:2 * GRP * N].rearrange("p (g u n) -> p g u n", g=2, u=GRP)
        atT = att[:, 2 * GRP * N:(2 * GRP + 2) * N].rearrange("p (s n) -> p s n", s=2)
        junk = [att[:, (2 * GRP + 2 + i) * N:(2 * GRP + 3 + i) * N] for i in range(3)]
        unread = [att[:, (2 * GRP + 2) * N + u * N // 2:(2 * GRP + 2) * N + (u + 1) * N // 2].bitcast(F16)
                  for u in range(GRP)]
        small_at = [(2 * GRP + 5) * N]

        def small(*shape, dt=F32):
            n = 1
            for k in shape:
                n *= k
            at = small_at[0]
            small_at[0] += (n + 7) // 8 * 8
            v = att[:, at:at + n]
            if dt != F32:
                v = v.bitcast(dt)
            if len(shape) == 2:
                v = v.rearrange("p (a b) -> p a b", a=shape[0])
            if len(shape) == 3:
                v = v.rearrange("p (a b c) -> p a b c", a=shape[0], b=shape[1])
            return v

        negmax, zsum, asum = small(2, GRP), small(2, GRP), small(2, GRP)
        target = small(GRP)
        bound = small(2, 2, GRP)
        cand = small(2, GRP)
        cand_i = small(GRP, dt=I32)
        cand_f = cand_i.bitcast(F32)
        mass = small(GRP)
        above, below = small(2, GRP), small(2, GRP)
        width = small(2, GRP)
        frac, t1, t2, t3 = small(GRP), small(GRP), small(GRP), small(GRP)
        seg_top = small(GRP, SEG, 8)
        seg_left = small(GRP, SEG * 8)
        window, csum, last, prod_w = (small(GRP, WIN) for _ in range(4))
        kept = small(GRP, WIN + 1)
        cut = small(GRP)
        ones_w = small(WIN)
        act_relu, act_sign = small(1), small(1)
        goal = small(GRP)
        unread_relu, unread_sign = (small(N // 2).bitcast(F16) for _ in range(2))
        flags, flagT = small(32), small(32)
        quad = small(4)
        flag_i = small(8, dt=I32)
        gl, gh, gm, gmass, gq = (small(1) for _ in range(5))
        g_up, g_dn = small(1), small(1)

        made = {}

        def sg(name):
            if name not in made:
                made[name] = ctx.enter_context(nc.semaphore(name))
            return made[name]

        block = ctx.enter_context(nc.Block())

        @block.sync
        def _(sp):
            def load(dst, src, name):
                sp.dma_start(dst, src).then_inc(sg(name), 16)

            def rows(ap):
                return ap.rearrange("(b p) d -> p b d", p=P)

            def stream(src, turn):
                for s in range(2):
                    if turn:
                        sp.wait_ge(sg(f"raw_free{s}"), NB // 2 * turn)
                    load(raw[s], src[s * P:(s + 1) * P, :], f"raw_in{s}")
                with sp.Fori(1, NB // 2) as i:
                    for s in range(2):
                        sp.wait_ge(sg(f"raw_free{s}"), i + NB // 2 * turn)
                        load(raw[s], src[bass.ds(i * (2 * P) + s * P, P), :], f"raw_in{s}")

            load(xb[:, :, :], rows(t["x"]), "x_in")
            load(winT1, t["W_inT1"].rearrange("(a p) d -> p a d", p=P), "w0_in")
            load(wout1, t["W_out1"].rearrange("(a p) d -> p a d", p=P), "w0_in")
            load(winT2, t["W_inT2"].rearrange("p (a d) -> p a d", a=2), "w0_in")
            load(bin1, t["b_in1"], "w0_in")
            load(bin2, t["b_in2"], "w0_in")
            load(wself1, t["W_self1"], "w0_in")
            load(w2cat[:, :, D:H], t["W_self2"].rearrange("(a p) d -> p a d", p=P), "w0_in")
            stream(t["adj"], 0)
            stream(t["adj"], 1)
            sp.wait_ge(sg("masked"), 1)
            for dst, n in ((g1, "g1"), (be1, "be1"), (bo1, "b_out1"), (bs1, "b_self1"),
                           (g2, "g2"), (be2, "be2"), (bo2, "b_out2"), (bs2, "b_self2")):
                load(dst, t[n].partition_broadcast(P), "vec0_in")
            load(wout2, t["W_out2"], "vec0_in")
            sp.wait_ge(sg("lin2"), 1)
            load(w1mix, t["W1"], "w1_in")
            load(w1mixT, t["W1T"], "w1_in")
            load(bmix, t["b"], "w1_in")
            stream(t["adjT"], 2)
            sp.wait_ge(sg("x1"), 1)
            load(w2mix, t["W2"], "w2_in")
            sp.wait_ge(sg("x2"), 1)
            load(w1a, t["L2_W1"], "w3_in")
            load(w2aT, t["L2_W2T"], "w3_in")
            load(w3aT, t["L2_W3T"], "w3_in")
            load(u1T, t["U1T"].rearrange("s p c -> p s c"), "w3_in")
            load(u2T, t["U2T"].rearrange("s p c -> p s c"), "w3_in")
            load(lng, t["ln_g"].partition_broadcast(P), "w3_in")
            load(lnb, t["ln_b"].partition_broadcast(P), "w3_in")
            sp.wait_ge(sg("xa_out"), NB * STEPS)
            load(wbuf[:, 0:D], t["L3_W"], "w4_in")
            load(wbuf[:, D:2 * D], t["L3_B"].partition_broadcast(P), "w4_in")
            for s in range(3):
                load(dist[:, s, :], t["adjT"][s * P:(s + 1) * P, :], f"dist_in{s}")
            with sp.Fori(1, NB // 3) as i:
                for s in range(3):
                    sp.wait_ge(sg(f"dist_in{s}"), i * 16)
                    load(dist[:, i * 3 + s, :], t["adjT"][bass.ds(i * (3 * P) + s * P, P), :], f"dist_in{s}")
            sp.wait_ge(sg("dist_in0"), NB // 3 * 16)
            load(dist[:, NB - 1, :], t["adjT"][(NB - 1) * P:NB * P, :], "dist_in0")
            sp.wait_ge(sg("x4"), 1)
            load(rows(out), zb[:, :, :], "out_done")
            sp.wait_ge(sg("out_done"), 16)

        @block.gpsimd
        def _(pool):
            nc.gpsimd.memset(ident[:, :], 0.0).then_inc(sg("zeroed"), 1)
            pool.wait_ge(sg("zeroed"), 1)
            nc.gpsimd.affine_select(out=ident[:, :], in_=ident[:, :], compare_op=ALU.not_equal, fill=1.0,
                                    base=0, pattern=[[-1, P]], channel_multiplier=1).then_inc(sg("consts"), 1)
            nc.gpsimd.memset(ones16[:, :], 1.0).then_inc(sg("consts"), 1)
            nc.gpsimd.memset(minus1[:, :], -1.0).then_inc(sg("consts"), 1)
            nc.gpsimd.memset(r_min[:, :], R_MIN).then_inc(sg("consts"), 1)

        @block.scalar
        def _(act):
            def root(name):
                act.wait_ge(sg(name + "_var"), 1)
                nc.scalar.activation(lnstd[:, :], lnvar[:, :], ACT.Sqrt).then_inc(sg(name + "_std"), 1)

            def copy(dst, src, name, count=1):
                act.wait_ge(sg(name), count)
                nc.scalar.activation(dst, src, ACT.Copy).then_inc(sg(name + "_out"), 1)

            def split_high(turn, done):
                with act.Fori(0, NB // 2) as i:
                    for s in range(2):
                        act.wait_ge(sg(f"raw_in{s}"), i * 16 + 16 * (NB // 2 * turn + 1))
                        nc.scalar.activation(big[:, 0, i * 2 + s, :], raw[s], ACT.Copy,
                                             scale=M_SCALE).then_inc(sg(done), 1)

            root("ln0")
            split_high(0, "high_adj")
            act.wait_ge(sg("wprod"), 1)
            act.wait_ge(sg("masked"), 1)
            nc.scalar.activation(wa1, ps[:, 0:H], ACT.Copy).then_inc(sg("wprod_out"), 1)
            nc.scalar.activation(w2cat[:, :, 0:D], ps[:, CH:CH + H].rearrange("p (a c) -> p a c", a=2),
                                 ACT.Copy).then_inc(sg("wprod_out"), 1)
            nc.scalar.activation(bw1, ps[:, 2 * CH:2 * CH + H], ACT.Copy).then_inc(sg("wprod_out"), 1)
            copy(arena[:, 0:N], ps[:, 0:N], "uT")
            copy(flat(pb), ps[:, N:2 * N], "h0T")
            root("ln1")
            for a in range(2):
                copy(hidT[:, a, :], ps[:, a * N:(a + 1) * N], "hidT", a + 1)
            root("ln2")
            root("ln3")
            act.wait_ge(sg("prod2"), 1)
            split_high(2, "high_adjT")
            copy(flat(pb), ps[:, 0:N], "h1T")
            copy(w1b, ps[:, N:N + D], "w1b")
            copy(node, ps[:, N + CH:N + CH + NB * KM].rearrange("p (b k) -> p b k", b=NB), "node")
            act.wait_ge(sg("y_pair"), 1)
            copy(flat(zb), ps[:, 0:N], "nodeb")
            root("ln4")
            copy(xfT, ps[:, 0:N], "xf1T")
            act.wait_ge(sg("z_xf1"), 1)
            copy(xfT, ps[:, 0:N], "xf2T")
            copy(wq, ps[:, 0:DA], "wq")
            for st in range(STEPS):
                xT = (pb, pa)[st]
                copy(flat(xT), ps[:, 0:N], "xaT", st + 1)
                copy(qT, ps[0:DA, 0:N], "qT", st + 1)
                copy(kT, ps[0:DA, N:2 * N], "kT", st + 1)

                def exps(g, u):
                    n = st * NB + g * GRP + u
                    act.wait_ge(sg("rowmax"), n + 1)
                    if g >= 2:
                        act.wait_ge(sg("a_turned"), n - 2 * GRP + 1)
                    nc.scalar.activation(ebuf[:, g % 2, u, :], ps[:, 0:N], ACT.Exp, bias=negmax[:, g % 2, u:u + 1],
                                         accum_out=zsum[:, g % 2, u:u + 1]).then_inc(sg("e_ready"), 1)

                def turned(g, u):
                    n = st * NB + g * GRP + u
                    act.wait_ge(sg("a_turned"), n + 1)
                    if n >= 2:
                        act.wait_ge(sg("ax"), n - 1)
                    nc.scalar.activation(atT[:, n % 2, :], ps[:, N:2 * N], ACT.Copy).then_inc(sg("at_out"), 1)

                def mixed(g, u):
                    n = st * NB + g * GRP + u
                    act.wait_ge(sg("ax"), n + 1)
                    nc.scalar.activation(xT[:, g * GRP + u, :], ps[:, N:N + D], ACT.Copy,
                                         scale=asum[:, g % 2, u:u + 1]).then_inc(sg("xa_out"), 1)

                def evaluate(g, k):
                    n = (st * NG + g) * EVALS + k
                    e, t = ebuf[:, g % 2, GRP - 1, :], cand_f[:, GRP - 1:GRP]
                    act.wait_ge(sg("candidate"), n + st * NG + g + 1)
                    nc.scalar.activation(unread_relu, e, ACT.Relu, scale=-1.0, bias=t,
                                         accum_out=act_relu).then_inc(sg("act_sums"), 1)
                    nc.scalar.activation(unread_sign, e, ACT.Sign, scale=-1.0, bias=t,
                                         accum_out=act_sign).then_inc(sg("act_sums"), 1)

                if st:
                    act.wait_ge(sg("z_xa1"), 1)
                for u in range(GRP):
                    exps(0, u)
                for g in range(NG + 1):
                    for k in range(EVALS):
                        if g < NG:
                            evaluate(g, k)
                        if g >= 1 and k < GRP:
                            turned(g - 1, k)
                        if g + 1 < NG and k < GRP:
                            exps(g + 1, k)
                        if g >= 1 and k < GRP:
                            mixed(g - 1, k)
            def inverse(n, slot, i=0):
                if not isinstance(n, int) or n >= 3:
                    act.wait_ge(sg("weights"), n - 2)
                act.wait_ge(sg(f"dist_in{slot}"), i * 16 + 16)
                nc.scalar.activation(sens[slot], dist[:, n, :], ACT.Ln, bias=r_min[:, 0:1]).then_inc(sg("ln_r"), 1)
                act.wait_ge(sg("ln_r"), n + 1)
                nc.scalar.activation(sens[slot], sens[slot], ACT.Exp, scale=-1.0).then_inc(sg("inverse"), 1)

            def sensitivity(n, slot):
                act.wait_ge(sg("neg_inverse"), n + 1)
                nc.scalar.activation(sens[slot], sens[slot], ACT.Square, bias=1.0).then_inc(sg("sens_sq"), 1)
                act.wait_ge(sg("sens_sq"), n + 1)
                nc.scalar.activation(sens[slot], sens[slot], ACT.Exp, scale=-2.0).then_inc(sg("sens"), 1)

            copy(flat(pb), ps[:, 0:N], "xaT", 3)
            act.wait_ge(sg("consts"), 4)
            nc.scalar.preload_act_table_set("natural_log_exp_and_others")
            inverse(0, 0)
            inverse(1, 1)
            root("ln5")
            root("ln6")
            nc.scalar.preload_act_table_set("natural_log_exp_and_others")
            inverse(2, 2)
            copy(flat(pb), ps[:, 0:N], "h3T")
            sensitivity(0, 0)
            with act.Fori(0, (NB - 4) // 3) as i:
                for s in range(3):
                    sensitivity(i * 3 + 1 + s, (s + 1) % 3)
                    inverse(i * 3 + 3 + s, s, i + 1)
            sensitivity(NB - 3, (NB - 3) % 3)
            inverse(NB - 1, (NB - 1) % 3, (NB - 1) // 3)
            sensitivity(NB - 2, (NB - 2) % 3)
            sensitivity(NB - 1, (NB - 1) % 3)
            copy(flat(pb), ps[:, 0:N], "x4T")

        @block.tensor
        def _(pe):
            def turn(src, col0, name):
                for b in range(NB):
                    mm = nc.tensor.transpose(ps[:, col0 + b * P:col0 + (b + 1) * P], src[:, b, :], ident[:, :])
                mm.then_inc(sg(name), 1)

            def linear(srcT, w, col0, name):
                for b in range(NB):
                    mm = nc.tensor.matmul(ps[:, col0 + b * P:col0 + (b + 1) * P], flat(srcT)[:, b * P:(b + 1) * P], w,
                                          start=True, stop=True)
                mm.then_inc(sg(name), 1)

            def tick(name):
                pe.wait_ge(sg(name + "_blk"), NB)
                nc.tensor.matmul(ps[0:1, 8 * CH - 1:8 * CH], ones16[0:1, 0:1], ones16[0:1, 0:1],
                                 start=True, stop=True).then_inc(sg(name), 1)

            def product(w, name):
                with pe.Fori(0, NB) as i:
                    for j in range(NB):
                        for n, (a, v) in enumerate(((0, 0), (0, 1), (1, 0))):
                            mm = nc.tensor.matmul(ps[:, bass.ds(i * WIDE, w)],
                                                  big[:, a, j, bass.ts(i, P)], pair[:, v, j, 0:w],
                                                  start=(j == 0 and n == 0), stop=(j == NB - 1 and n == 2))
                    mm.then_inc(sg(name + "_blk"), 1)
                tick(name)

            pe.wait_ge(sg("consts"), 4)
            with pe.Fori(0, NB) as i:
                pe.wait_ge(sg("low_adj"), i + 1)
                for c in range(NCH):
                    for a in range(2):
                        mm = nc.tensor.matmul(ps[:, (c + 4 * a) * CH:(c + 4 * a + 1) * CH], ones16[:, :],
                                              big[:, a, i, c * CH:(c + 1) * CH], start=False, stop=False,
                                              skip_group_check=True)
                mm.then_inc(sg("colsum_mm"), 1)
            pe.wait_ge(sg("w0_in"), 16 * 7)
            pe.wait_ge(sg("vec0_in"), 16 * 9)
            pe.wait_ge(sg("bin_rep"), 1)
            pe.wait_ge(sg("thresholds"), 1)
            for a in range(2):
                nc.tensor.matmul(ps[:, 0:H], winT1[:, a, :], wout1[:, a, :], start=(a == 0), stop=(a == 1))
            for a in range(2):
                nc.tensor.matmul(ps[:, CH + a * D:CH + (a + 1) * D], winT2[:, a, :], wout2, start=True, stop=True)
            for a in range(2):
                mm = nc.tensor.matmul(ps[:, 2 * CH:2 * CH + H], bin1_rep[:, a, :], wout1[:, a, :],
                                      start=(a == 0), stop=(a == 1))
            mm.then_inc(sg("wprod"), 1)
            pe.wait_ge(sg("wprod_out"), 3)
            pe.wait_ge(sg("masked"), 1)
            pe.wait_ge(sg("h0_pair"), 1)
            product(D + 1, "prod1")
            pe.wait_ge(sg("u"), 1)
            turn(zb, 0, "uT")
            turn(pa, N, "h0T")
            pe.wait_ge(sg("uT_out"), 1)
            pe.wait_ge(sg("h0T_out"), 1)
            for b in range(NB):
                o = ps[:, b * H:(b + 1) * H]
                nc.tensor.matmul(o, arena[:, b * P:(b + 1) * P], wa1, start=True, stop=False)
                mm = nc.tensor.matmul(o, flat(pb)[:, b * P:(b + 1) * P], wself1, start=False, stop=True)
            mm.then_inc(sg("lin1"), 1)
            pe.wait_ge(sg("hid"), 1)
            for a in range(2):
                for b in range(NB):
                    mm = nc.tensor.transpose(ps[:, a * N + b * P:a * N + (b + 1) * P], hid[:, b, a * P:(a + 1) * P],
                                             ident[:, :])
                mm.then_inc(sg("hidT"), 1)
            pe.wait_ge(sg("hidT_out"), 2)
            for b in range(NB):
                o = ps[:, b * H:(b + 1) * H]
                nc.tensor.matmul(o, hidT[:, 0, b * P:(b + 1) * P], w2cat[:, 0, :], start=True, stop=False)
                nc.tensor.matmul(ps[:, b * H:b * H + D], bin2_rep, wout2, start=False, stop=False)
                mm = nc.tensor.matmul(o, hidT[:, 1, b * P:(b + 1) * P], w2cat[:, 1, :], start=False, stop=True)
            mm.then_inc(sg("lin2"), 1)
            pe.wait_ge(sg("p_pair"), 1)
            product(D, "prod2")
            pe.wait_ge(sg("h1"), 1)
            turn(pa, 0, "h1T")
            pe.wait_ge(sg("w1_in"), 16 * 3)
            nc.tensor.matmul(ps[:, N:N + D], w1mixT, bmix, start=True, stop=True).then_inc(sg("w1b"), 1)
            pe.wait_ge(sg("h1T_out"), 1)
            for b in range(NB):
                mm = nc.tensor.matmul(ps[:, N + CH + b * KM:N + CH + (b + 1) * KM], flat(pb)[:, b * P:(b + 1) * P],
                                      w1mix, start=True, stop=True)
            mm.then_inc(sg("node"), 1)
            pe.wait_ge(sg("w1b_out"), 1)
            pe.wait_ge(sg("node_out"), 1)
            pe.wait_ge(sg("w2_in"), 16)
            for b in range(NB):
                if b >= 2:
                    pe.wait_ge(sg("mix_used"), b - 1)
                for c in range(NCH):
                    o = (b % 2 * NCH + c) * CH
                    mm = nc.tensor.matmul(ps[:, o:o + CH], flat(pb)[:, b * P:(b + 1) * P],
                                          w2mix[:, c * CH:(c + 1) * CH], start=True, stop=True)
                mm.then_inc(sg("mix_mm"), 1)
            pe.wait_ge(sg("mix_used"), NB)
            linear(pb, w1b, 0, "nodeb")
            pe.wait_ge(sg("nodeb_out"), 1)
            pe.wait_ge(sg("y_pair"), 1)
            pe.wait_ge(sg("adjT_split"), 1)
            product(D, "prod3")
            pe.wait_ge(sg("h2_pair"), 1)
            product(D + 1, "prod4")
            pe.wait_ge(sg("xf1"), 1)
            turn(pb, 0, "xf1T")
            pe.wait_ge(sg("xf1T_out"), 1)
            pe.wait_ge(sg("w3_in"), 16 * 7)
            for b in range(NB):
                mm = nc.tensor.matmul(ps[:, N + b * P:N + (b + 1) * P], xfT[:, b * P:(b + 1) * P], u1T[:, 0, :],
                                      start=True, stop=True)
            mm.then_inc(sg("zxf1"), 1)
            pe.wait_ge(sg("z_xf1"), 1)
            pe.wait_ge(sg("xf1_pair"), 1)
            product(D, "prod5")
            pe.wait_ge(sg("xf2"), 1)
            turn(xf2, 0, "xf2T")
            pe.wait_ge(sg("xf2T_out"), 1)
            for b in range(NB):
                mm = nc.tensor.matmul(ps[:, N + b * P:N + (b + 1) * P], xfT[:, b * P:(b + 1) * P], u1T[:, 1, :],
                                      start=True, stop=True)
            mm.then_inc(sg("zxf2"), 1)
            nc.tensor.matmul(ps[:, 0:DA], w1a, w2aT, start=True, stop=True).then_inc(sg("wq"), 1)
            pe.wait_ge(sg("wq_out"), 1)
            pe.wait_ge(sg("z_xf2"), 1)
            for st in range(STEPS):
                xa, xT = ((pa, pb), (pb, pa))[st]
                turn(xa, 0, "xaT")
                pe.wait_ge(sg("xaT_out"), st + 1)
                for c in range(NCH):
                    mm = nc.tensor.matmul(ps[0:DA, c * CH:(c + 1) * CH], wq, flat(xT)[:, c * CH:(c + 1) * CH],
                                          start=True, stop=True)
                mm.then_inc(sg("qT"), 1)
                for c in range(NCH):
                    mm = nc.tensor.matmul(ps[0:DA, N + c * CH:N + (c + 1) * CH], w3aT, flat(xT)[:, c * CH:(c + 1) * CH],
                                          start=True, stop=True)
                mm.then_inc(sg("kT"), 1)
                pe.wait_ge(sg("qT_out"), st + 1)
                pe.wait_ge(sg("kT_out"), st + 1)
                if st:
                    linear(xT, u2T[:, 0, :], N, "zxa1")
                    pe.wait_ge(sg("z_xa1"), 1)

                def logits(g, u):
                    n = st * NB + g * GRP + u
                    if n:
                        pe.wait_ge(sg("e_ready"), n)
                    for c in range(NCH):
                        mm = nc.tensor.matmul(ps[:, c * CH:(c + 1) * CH], qT[:, (g * GRP + u) * P:(g * GRP + u + 1) * P],
                                              kT[:, c * CH:(c + 1) * CH], start=True, stop=True)
                    mm.then_inc(sg("logits"), 1)

                def turn_a(g, u):
                    n = st * NB + g * GRP + u
                    if u == 0:
                        pe.wait_ge(sg("a_ready"), st * NG + g + 1)
                    if n:
                        pe.wait_ge(sg("xa_out"), n)
                    for j in range(NB):
                        mm = nc.tensor.transpose(ps[:, N + j * P:N + (j + 1) * P],
                                                 ebuf[:, g % 2, u, j * P:(j + 1) * P], ident[:, :])
                    mm.then_inc(sg("a_turned"), 1)

                def mix_a(g, u):
                    n = st * NB + g * GRP + u
                    pe.wait_ge(sg("at_out"), n + 1)
                    for j in range(NB):
                        mm = nc.tensor.matmul(ps[:, N:N + D], atT[:, n % 2, j * P:(j + 1) * P], xa[:, j, :],
                                              start=(j == 0), stop=(j == NB - 1))
                    mm.then_inc(sg("ax"), 1)

                for u in range(GRP):
                    logits(0, u)
                for g in range(NG + 1):
                    for u in range(GRP):
                        if g >= 1:
                            turn_a(g - 1, u)
                        if g + 1 < NG:
                            logits(g + 1, u)
                        if g >= 1:
                            mix_a(g - 1, u)
                pe.wait_ge(sg("xa_out"), NB * (st + 1))
            turn(pa, 0, "xaT")
            pe.wait_ge(sg("xaT_out"), 3)
            linear(pb, u2T[:, 1, :], N, "zxa2")
            pe.wait_ge(sg("h3"), 1)
            turn(pa, 0, "h3T")
            pe.wait_ge(sg("h3T_out"), 1)
            pe.wait_ge(sg("w4_in"), 16 * 2)
            linear(pb, wbuf[:, 0:D], N, "msg")
            pe.wait_ge(sg("msg_b"), 1)
            for j in range(NB):
                pe.wait_ge(sg("weights"), j + 1)
                for c in range(NCH):
                    mm = nc.tensor.matmul(ps[:, c * CH:(c + 1) * CH], zb[:, j, :], dist[:, j, c * CH:(c + 1) * CH],
                                          start=(j == 0), stop=(j == NB - 1))
            mm.then_inc(sg("x4T"), 1)
            pe.wait_ge(sg("x4T_out"), 1)
            turn(pb, N, "prod6")

        @block.vector
        def _(dve):
            v = nc.vector
            done = [0]

            def step(ins):
                ins.then_inc(sg("dve_step"), 1)
                done[0] += 1
                dve.wait_ge(sg("dve_step"), done[0])

            def tell(ins, name, count=1):
                ins.then_inc(sg(name), 1)
                dve.wait_ge(sg(name), count)

            def layernorm(src, dst, tmp, w, name, gamma=None, beta=None, relu=True):
                step(v.tensor_reduce(lnsum[:, :], src, AX_X, ALU.add))
                step(v.tensor_scalar(lnsum[:, :], lnsum[:, :], 1.0 / w, None, ALU.mult))
                step(v.tensor_tensor(dst, src, over(lnsum[:, :], w), ALU.subtract))
                step(v.tensor_tensor(tmp, dst, dst, ALU.mult))
                step(v.tensor_reduce(lnvar[:, :], tmp, AX_X, ALU.add))
                tell(v.tensor_scalar(lnvar[:, :], lnvar[:, :], 1.0 / w, LN_EPS, ALU.mult, ALU.add), name + "_var")
                dve.wait_ge(sg(name + "_std"), 1)
                step(v.reciprocal(lninv[:, :], lnstd[:, :]))
                step(v.tensor_tensor(dst, dst, over(lninv[:, :], w), ALU.mult))
                if gamma is not None:
                    step(v.tensor_tensor(dst, dst, along(gamma, w), ALU.mult))
                    step(v.tensor_tensor(dst, dst, along(beta, w), ALU.add))
                if relu:
                    step(v.tensor_scalar(dst, dst, 0.0, None, ALU.max))

            def make_pair(src, name, ones=False):
                step(v.tensor_scalar(pair[:, 0, :, 0:D], src, V_SCALE, None, ALU.mult))
                if ones:
                    step(v.memset(pair[:, 0, :, D:D + 1], 1.0))
                    step(v.memset(pair[:, 1, :, D:D + 1], 0.0))
                tell(v.scalar_tensor_tensor(out=pair[:, 1, :, 0:D], in0=src, scalar=V_SCALE, in1=pair[:, 0, :, 0:D],
                                            op0=ALU.mult, op1=ALU.subtract), name)

            def split_low(high, low, base):
                with dve.Fori(0, NB // 2) as i:
                    for s in range(2):
                        dve.wait_ge(sg(high), i * 2 + s + 1)
                        v.scalar_tensor_tensor(out=big[:, 1, i * 2 + s, :], in0=raw[s], scalar=M_SCALE,
                                               in1=big[:, 0, i * 2 + s, :], op0=ALU.mult,
                                               op1=ALU.subtract).then_inc(sg(low), 1)
                        dve.wait_ge(sg(low), i * 2 + s + 1)
                        v.memset(t_free[s][:, :], 0.0).then_inc(sg(f"raw_free{s}"), 1)

            t_free = [sb(f"t_free{s}", [P, 1]) for s in range(2)]

            step(v.memset(ps[:, :], 0.0))
            dve.wait_ge(sg("x_in"), 16)
            layernorm(xb[:, :, :], pa[:, :, :], zb[:, :, :], D, "ln0")
            make_pair(pa[:, :, :], "h0_pair", ones=True)
            split_low("high_adj", "low_adj", 0)
            dve.wait_ge(sg("w0_in"), 16 * 7)
            dve.wait_ge(sg("colsum_mm"), NB)
            step(v.tensor_scalar(tail, ps[:, 0:N], 1.0 / M_SCALE, EPS, ALU.mult, ALU.add))
            step(v.scalar_tensor_tensor(out=tail, in0=ps[:, N:2 * N], scalar=1.0 / M_SCALE, in1=tail,
                                        op0=ALU.mult, op1=ALU.add))
            dve.wait_ge(sg("consts"), 4)
            step(v.tensor_tensor(zb[:, :, :], blocks(tail), along(ident[:, :], D), ALU.mult))
            step(v.tensor_reduce(colsum[:, :], zb[:, :, :], AX_X, ALU.add))
            tell(v.tensor_scalar(tail, tail, THRESH, None, ALU.mult), "thresholds")
            with dve.Fori(0, NB // 2) as i:
                for s in range(2):
                    dve.wait_ge(sg(f"raw_in{s}"), i * 16 + 16 * (NB // 2 + 1))
                    v.tensor_tensor(mask16, raw[s], tail, ALU.is_gt).then_inc(sg(f"raw_free{s}"), 1)
                    dve.wait_ge(sg(f"raw_free{s}"), i + NB // 2 + 1)
                    for a in range(2):
                        m = big[:, a, i * 2 + s, :]
                        v.tensor_tensor(m, m, mask16, ALU.mult).then_inc(sg("mask_mul"), 1)
                    dve.wait_ge(sg("mask_mul"), i * 4 + s * 2 + 2)
            for a in range(2):
                step(v.tensor_scalar(bin1_rep[:, a, :], zb[:, 0, :], 0.0, bin1[:, a:a + 1], ALU.mult, ALU.add))
            tell(v.memset(t_free[0][:, :], 0.0), "masked")
            tell(v.tensor_scalar(bin2_rep, zb[:, 0, :], 0.0, bin2, ALU.mult, ALU.add), "bin_rep")
            dve.wait_ge(sg("prod1"), 1)
            step(v.tensor_scalar(wsum[:, :], wide[:, :, D], 1.0 / M_SCALE, None, ALU.mult))
            step(v.tensor_scalar(no_edge[:, :], wsum[:, :], 0.0, None, ALU.is_le))
            step(v.scalar_tensor_tensor(out=inv_w[:, :], in0=colsum[:, :], scalar=EPS, in1=wsum[:, :],
                                        op0=ALU.mult, op1=ALU.add))
            step(v.reciprocal(inv_w[:, :], inv_w[:, :]))
            step(v.tensor_tensor(bias_w[:, :], wsum[:, :], inv_w[:, :], ALU.mult))
            step(v.tensor_tensor(bias_w[:, :], bias_w[:, :], no_edge[:, :], ALU.add))
            step(v.tensor_scalar(inv_w[:, :], inv_w[:, :], UNSCALE, None, ALU.mult))
            dve.wait_ge(sg("vec0_in"), 16 * 9)
            dve.wait_ge(sg("wprod_out"), 3)
            step(v.tensor_tensor(zb[:, :, :], pa[:, :, :], over(no_edge[:, :], D), ALU.mult))
            step(v.tensor_tensor(pb[:, :, :], wide[:, :, 0:D], over(inv_w[:, :], D), ALU.mult))
            tell(v.tensor_tensor(zb[:, :, :], zb[:, :, :], pb[:, :, :], ALU.add), "u")
            step(v.tensor_tensor(bo1, bo1, bs1, ALU.add))
            step(v.tensor_tensor(bo2, bo2, bs2, ALU.add))
            step(v.tensor_tensor(hid, along(bw1, H), over(bias_w[:, :], H), ALU.mult))
            step(v.tensor_tensor(hid, hid, along(bo1, H), ALU.add))
            dve.wait_ge(sg("lin1"), 1)
            step(v.tensor_tensor(hid, hid, wide, ALU.add))
            layernorm(hid, hid, blocks(arena[:, 0:2 * N]), H, "ln1", g1, be1)
            tell(v.memset(t_free[0][:, :], 0.0), "hid")
            dve.wait_ge(sg("lin2"), 1)
            step(v.tensor_copy(pb[:, :, :], wide[:, :, 0:D]))
            step(v.tensor_tensor(zb[:, :, :], wide[:, :, D:H], along(bo2, D), ALU.add))
            make_pair(pb[:, :, :], "p_pair")
            step(v.tensor_tensor(pb[:, :, :], pb[:, :, :], over(no_edge[:, :], D), ALU.mult))
            step(v.tensor_tensor(zb[:, :, :], zb[:, :, :], pb[:, :, :], ALU.add))
            dve.wait_ge(sg("prod2"), 1)
            step(v.tensor_tensor(pa[:, :, :], wide[:, :, 0:D], over(inv_w[:, :], D), ALU.mult))
            step(v.tensor_tensor(pa[:, :, :], pa[:, :, :], zb[:, :, :], ALU.add))
            layernorm(pa[:, :, :], pa[:, :, :], zb[:, :, :], D, "ln2", g2, be2)
            tell(v.tensor_tensor(xb[:, :, :], xb[:, :, :], pa[:, :, :], ALU.add), "x1")
            layernorm(xb[:, :, :], pa[:, :, :], zb[:, :, :], D, "ln3")
            tell(v.memset(t_free[0][:, :], 0.0), "h1")
            split_low("high_adjT", "low_adjT", 2)
            tell(v.memset(t_free[0][:, :], 0.0), "adjT_split")
            dve.wait_ge(sg("node_out"), 1)
            with dve.Fori(0, NB // 2) as i:
                for s in range(2):
                    b = i * 2 + s
                    dve.wait_ge(sg("mix_mm"), b + 1)
                    for k in range(KM):
                        o = s * N + k * D
                        src, w = ps[:, o:o + D], node[:, b, k:k + 1]
                        if k == 0:
                            ins = v.tensor_scalar(zb[:, b, :], src, w, None, ALU.mult)
                        else:
                            ins = v.scalar_tensor_tensor(out=zb[:, b, :], in0=src, scalar=w, in1=zb[:, b, :],
                                                         op0=ALU.mult, op1=ALU.add)
                        ins.then_inc(sg("mix_add"), 1)
                        dve.wait_ge(sg("mix_add"), b * KM + k + 1)
                    v.memset(t_free[0][:, :], 0.0).then_inc(sg("mix_used"), 1)
            make_pair(zb[:, :, :], "y_pair")
            dve.wait_ge(sg("nodeb_out"), 1)
            dve.wait_ge(sg("prod3"), 1)
            step(v.scalar_tensor_tensor(out=pa[:, :, :], in0=wide[:, :, 0:D], scalar=UNSCALE, in1=zb[:, :, :],
                                        op0=ALU.mult, op1=ALU.add))
            tell(v.scalar_tensor_tensor(out=xb[:, :, :], in0=pa[:, :, :], scalar=0.0, in1=xb[:, :, :],
                                        op0=ALU.max, op1=ALU.add), "x2")
            layernorm(xb[:, :, :], pa[:, :, :], zb[:, :, :], D, "ln4")
            step(v.tensor_copy(zb[:, :, :], pa[:, :, :]))
            make_pair(pa[:, :, :], "h2_pair", ones=True)
            dve.wait_ge(sg("prod4"), 1)
            step(v.tensor_scalar(wsum[:, :], wide[:, :, D], 1.0 / M_SCALE, 1.0, ALU.mult, ALU.add))
            step(v.reciprocal(wsum[:, :], wsum[:, :]))
            step(v.scalar_tensor_tensor(out=pb[:, :, :], in0=wide[:, :, 0:D], scalar=UNSCALE, in1=pa[:, :, :],
                                        op0=ALU.mult, op1=ALU.add))
            tell(v.tensor_tensor(pb[:, :, :], pb[:, :, :], over(wsum[:, :], D), ALU.mult), "xf1")
            make_pair(pb[:, :, :], "xf1_pair")
            dve.wait_ge(sg("zxf1"), 1)
            tell(v.tensor_tensor(zb[:, :, :], zb[:, :, :], high4, ALU.add), "z_xf1")
            dve.wait_ge(sg("prod5"), 1)
            step(v.scalar_tensor_tensor(out=xf2, in0=wide[:, :, 0:D], scalar=UNSCALE, in1=pb[:, :, :],
                                        op0=ALU.mult, op1=ALU.add))
            tell(v.tensor_tensor(xf2, xf2, over(wsum[:, :], D), ALU.mult), "xf2")
            dve.wait_ge(sg("zxf2"), 1)
            tell(v.tensor_tensor(zb[:, :, :], zb[:, :, :], high4, ALU.add), "z_xf2")
            step(v.memset(ones_w, 1.0))
            step(v.memset(kept[:, :, WIN:WIN + 1], 0.0))
            step(v.memset(flags, 0.0))

            def bc2(a):
                return a.unsqueeze(1).to_broadcast([P, 2, GRP])

            def row_max(st, g, u, n_const, k):
                dve.wait_ge(sg("logits"), k + (n_const + 1))
                v.tensor_reduce(negmax[:, g % 2, bass.ds(k, 1)] if u is None else negmax[:, g % 2, u:u + 1],
                                ps[:, 0:N], AX_X, ALU.max, negate=True).then_inc(sg("rowmax"), 1)

            def evaluations(g, count, before, produce):
                with dve.Fori(0, count) as k:
                    for u in range(GRP - 1):
                        e = ebuf[:, g % 2, u, :]
                        if u == GRP - 2:
                            dve.wait_ge(sg("act_sums"), k * 2 + 2 * (before + 1))
                            v.tensor_scalar(act_sign, act_sign, -0.5, -0.5 * N, ALU.mult, ALU.add)
                        v.scalar_tensor_tensor(out=unread[u], in0=e, scalar=cand_f[:, u:u + 1], in1=e,
                                               op0=ALU.is_gt, op1=ALU.mult, accum_out=mass[:, u:u + 1])
                    dve.drain()
                    v.scalar_tensor_tensor(out=mass[:, GRP - 1:GRP], in0=cand_f[:, GRP - 1:GRP],
                                           scalar=act_sign, in1=act_relu, op0=ALU.mult, op1=ALU.add)
                    v.tensor_scalar(bound[:, :, 1, :], bound[:, :, 1, :], 0.7, None, ALU.mult)
                    dve.drain()
                    v.tensor_tensor(cand[:, 1, :], mass, goal, ALU.subtract)
                    dve.drain()
                    v.tensor_scalar(above, bc2(cand[:, 1, :]), 0.0, None, ALU.is_ge)
                    v.tensor_scalar(below, bc2(cand[:, 1, :]), 0.0, None, ALU.is_lt)
                    dve.drain()
                    v.copy_predicated(bound[:, 0, :, :], above.bitcast(I32), cand)
                    v.copy_predicated(bound[:, 1, :, :], below.bitcast(I32), cand)
                    dve.drain()
                    v.tensor_tensor(width, bound[:, 1, :, :], bound[:, 0, :, :], ALU.subtract)
                    v.scalar_tensor_tensor(out=frac, in0=cand_f, scalar=-6.0, in1=bound[:, 0, 1, :],
                                           op0=ALU.mult, op1=ALU.subtract)
                    dve.drain()
                    v.reciprocal(t1, width[:, 1, :])
                    dve.drain()
                    v.tensor_tensor(frac, frac, t1, ALU.mult)
                    dve.drain()
                    v.tensor_scalar(frac, frac, 0.98, 0.02, ALU.min, ALU.max)
                    dve.drain()
                    v.tensor_tensor(frac, frac, width[:, 0, :], ALU.mult)
                    dve.drain()
                    v.tensor_tensor(cand[:, 0, :], frac, bound[:, 0, 0, :], ALU.add)
                    dve.drain()
                    v.tensor_copy(cand_i, cand[:, 0, :]).then_inc(sg("candidate"), 1)
                    if produce is not None:
                        row_max(None, g + 1, None, produce, k)
                    dve.drain()

            def general(g):
                with dve.Fori(0, GRP) as u:
                    e = ebuf[:, g % 2, u, :]
                    tg, zs = target[:, bass.ds(u, 1)], zsum[:, g % 2, bass.ds(u, 1)]
                    v.tensor_scalar(gl, zs, 0.0999 / N, None, ALU.mult)
                    v.memset(gh, 1.0)
                    v.memset(gmass, 0.0)
                    dve.drain()
                    with dve.Fori(0, HALVINGS) as _:
                        v.tensor_scalar(gm, gl, gh[:, 0:1], 0.5, ALU.add, ALU.mult)
                        dve.drain()
                        v.scalar_tensor_tensor(out=junk[0], in0=e, scalar=gm[:, 0:1], in1=e, op0=ALU.is_gt, op1=ALU.mult,
                                               accum_out=gq)
                        dve.drain()
                        v.tensor_tensor(g_up, gq, tg, ALU.is_ge)
                        v.tensor_tensor(g_dn, gq, tg, ALU.is_lt)
                        dve.drain()
                        v.copy_predicated(gl, g_up.bitcast(I32), gm)
                        v.copy_predicated(gh, g_dn.bitcast(I32), gm)
                        v.copy_predicated(gmass, g_dn.bitcast(I32), gq)
                        dve.drain()
                    v.tensor_tensor(gq, tg, gmass, ALU.subtract)
                    v.reciprocal(gm, gh)
                    v.tensor_scalar(junk[0], e, gh[:, 0:1], None, ALU.is_equal)
                    v.memset(junk[1], 1.0)
                    dve.drain()
                    v.tensor_scalar(gq, gq, gm[:, 0:1], 1.0, ALU.mult, ALU.add)
                    v.tensor_tensor_scan(junk[2], junk[1], junk[0], 0.0, ALU.mult, ALU.add)
                    dve.drain()
                    v.scalar_tensor_tensor(out=junk[0], in0=junk[2], scalar=gq[:, 0:1], in1=junk[0],
                                           op0=ALU.is_lt, op1=ALU.mult)
                    dve.drain()
                    v.scalar_tensor_tensor(out=junk[0], in0=e, scalar=gh[:, 0:1], in1=junk[0],
                                           op0=ALU.is_gt, op1=ALU.add)
                    dve.drain()
                    v.scalar_tensor_tensor(out=e, in0=e, scalar=1.0, in1=junk[0], op0=ALU.mult, op1=ALU.mult,
                                           accum_out=asum[:, g % 2, bass.ds(u, 1)])
                    dve.drain()

            def search(st, g):
                base = st * NB + g * GRP
                dve.wait_ge(sg("e_ready"), base + GRP)
                zs = zsum[:, g % 2, :]
                step(v.tensor_scalar(target, zs, TOP_P, None, ALU.mult))
                step(v.tensor_scalar(t1, zs, 0.0999 / N, None, ALU.mult))
                step(v.tensor_copy(bound[:, 0, 0, :], t1.bitcast(I32)))
                step(v.memset(bound[:, 1, 0, :], ONE_BITS))
                step(v.tensor_tensor(bound[:, 0, 1, :], zs, target, ALU.subtract))
                step(v.tensor_scalar(bound[:, 1, 1, :], target, -1.0, None, ALU.mult))
                step(v.tensor_scalar(cand[:, 0, :], bound[:, 0, 0, :], 0.75, 0.25 * ONE_BITS, ALU.mult, ALU.add))
                v.tensor_scalar(goal[:, 0:GRP - 1], zs[:, 0:GRP - 1], TOP_P - 1e-5, None, ALU.mult)
                v.tensor_scalar(goal[:, GRP - 1:GRP], zs[:, GRP - 1:GRP], TOP_P - 3e-5 - 1.0, None, ALU.mult)
                before = (st * NG + g) * EVALS
                v.tensor_copy(cand_i, cand[:, 0, :]).then_inc(sg("candidate"), 1)
                dve.drain()
                if g + 1 < NG:
                    evaluations(g, GRP, before, base + GRP)
                    evaluations(g, EVALS - GRP, before + GRP, None)
                else:
                    evaluations(g, EVALS, before, None)
                step(v.tensor_copy(cand_i, bound[:, 1, 0, :]))
                for u in range(GRP):
                    e = ebuf[:, g % 2, u, :]
                    v.scalar_tensor_tensor(out=junk[u % 2], in0=e, scalar=cand_f[:, u:u + 1], in1=e,
                                           op0=ALU.is_le, op1=ALU.mult, accum_out=mass[:, u:u + 1])
                    dve.drain()
                    for q in range(SEG):
                        v.max(seg_top[:, u, q, :], junk[u % 2][:, q * (N // SEG):(q + 1) * (N // SEG)])
                dve.drain()
                for u in range(GRP):
                    v.max(window[:, u, 0:8], seg_top[:, u, :, :].rearrange("p s c -> p (s c)"))
                dve.drain()
                for u in range(GRP):
                    v.match_replace(seg_left[:, u, :], window[:, u, 0:8],
                                    seg_top[:, u, :, :].rearrange("p s c -> p (s c)"), 0.0)
                v.tensor_tensor(t1, zs, mass, ALU.subtract)
                dve.drain()
                for u in range(GRP):
                    v.max(window[:, u, 8:WIN], seg_left[:, u, :])
                dve.drain()
                for u in range(GRP):
                    v.tensor_tensor_scan(csum[:, u, :], ones_w, window[:, u, :], t1[:, u:u + 1], ALU.mult, ALU.add)
                dve.drain()
                step(v.tensor_tensor(csum, csum, window, ALU.subtract))
                step(v.tensor_tensor(kept[:, :, 0:WIN], csum, target.unsqueeze(2).to_broadcast([P, GRP, WIN]),
                                     ALU.is_lt))
                step(v.tensor_tensor(last, kept[:, :, 0:WIN], kept[:, :, 1:WIN + 1], ALU.subtract))
                step(v.tensor_tensor(prod_w, last, window, ALU.mult))
                step(v.tensor_reduce(cut, prod_w, AX_X, ALU.add))
                step(v.tensor_tensor(prod_w[:, :, 0:WIN - 1], last[:, :, 0:WIN - 1], window[:, :, 1:WIN], ALU.mult))
                v.tensor_reduce(t2, prod_w[:, :, 0:WIN - 1], AX_X, ALU.add)
                step(v.tensor_reduce(t1, seg_top[:, :, :, 7], AX_X, ALU.max))
                v.tensor_tensor(t1, t1, cut, ALU.is_ge)
                v.tensor_scalar(t3, kept[:, :, 0], -1.0, 1.0, ALU.mult, ALU.add)
                step(v.tensor_tensor(t2, t2, cut, ALU.is_equal))
                v.tensor_tensor(t3, t3, t1, ALU.add)
                step(v.tensor_tensor(t2, t2, kept[:, :, WIN - 1], ALU.add))
                step(v.tensor_tensor(t2, t2, t3, ALU.add))
                step(v.tensor_reduce(flags[:, 0:1], t2, AX_X, ALU.max))
                step(v.transpose(flagT, flags))
                step(v.tensor_reduce(t3[:, 0:1], flagT, AX_X, ALU.max))
                for q in range(4):
                    step(v.tensor_copy(quad[0:1, q:q + 1], t3[32 * q:32 * q + 1, 0:1]))
                step(v.tensor_reduce(flag_i[0:1, 0:1], quad[0:1, :], AX_X, ALU.max))
                if st * NG + g >= 2:
                    dve.wait_ge(sg("xa_out"), base - GRP)
                undecided = dve.value_load(flag_i[0:1, 0:1], min_val=0, max_val=4)
                with dve.If(undecided > 0):
                    general(g)
                with dve.Else():
                    for u in range(GRP):
                        e = ebuf[:, g % 2, u, :]
                        v.scalar_tensor_tensor(out=e, in0=e, scalar=cut[:, u:u + 1], in1=e, op0=ALU.is_ge,
                                               op1=ALU.mult, accum_out=asum[:, g % 2, u:u + 1])
                    dve.drain()
                step(v.tensor_scalar(asum[:, g % 2, :], asum[:, g % 2, :], SUM_MIN, None, ALU.max))
                tell(v.reciprocal(asum[:, g % 2, :], asum[:, g % 2, :]), "a_ready", st * NG + g + 1)

            for st in range(STEPS):
                if st:
                    dve.wait_ge(sg("zxa1"), 1)
                    tell(v.tensor_tensor(zb[:, :, :], zb[:, :, :], high4, ALU.add), "z_xa1")
                for u in range(GRP):
                    row_max(st, 0, u, st * NB + u, 0)
                for g in range(NG):
                    search(st, g)
            dve.wait_ge(sg("zxa2"), 1)
            step(v.tensor_tensor(zb[:, :, :], zb[:, :, :], high4, ALU.add))
            layernorm(zb[:, :, :], zb[:, :, :], pa[:, :, :], D, "ln5", lng, lnb, relu=False)
            tell(v.tensor_tensor(xb[:, :, :], xb[:, :, :], zb[:, :, :], ALU.add), "x3")
            layernorm(xb[:, :, :], pa[:, :, :], zb[:, :, :], D, "ln6")
            tell(v.memset(t_free[0][:, :], 0.0), "h3")
            dve.wait_ge(sg("w4_in"), 16 * 2)
            dve.wait_ge(sg("msg"), 1)
            tell(v.tensor_tensor(zb[:, :, :], high4, along(wbuf[:, D:2 * D], D), ALU.add), "msg_b")

            def neg_inverse(n, slot):
                dve.wait_ge(sg("inverse"), n + 1)
                v.tensor_tensor(ratio, dist[:, n, :], sens[slot], ALU.mult)
                dve.drain()
                v.scalar_tensor_tensor(out=sens[slot], in0=ratio, scalar=-2.0, in1=sens[slot], op0=ALU.add,
                                       op1=ALU.mult).then_inc(sg("neg_inverse"), 1)

            def weigh(n, slot):
                dve.wait_ge(sg("sens"), n + 1)
                v.scalar_tensor_tensor(out=dist[:, n, :], in0=dist[:, n, :], scalar=1.0, in1=sens[slot],
                                       op0=ALU.is_lt, op1=ALU.mult).then_inc(sg("weights"), 1)

            neg_inverse(0, 0)
            with dve.Fori(0, (NB - 1) // 3) as i:
                for s in range(3):
                    dve.drain()
                    neg_inverse(i * 3 + s + 1, (s + 1) % 3)
                    weigh(i * 3 + s, s)
            weigh(NB - 1, (NB - 1) % 3)
            dve.wait_ge(sg("prod6"), 1)
            tell(v.tensor_tensor(zb[:, :, :], high4, xb[:, :, :], ALU.add), "x4")


def kernel(**inputs):
    import numpy as np
    import concourse.bacc as bacc
    from concourse.bass_utils import run_bass_kernel_spmd as run

    a = {k: np.asarray(v) for k, v in inputs.items()}
    laid = {
        "x": a["x"], "adj": a["adj"], "adjT": a["adj"].T,
        "W_inT1": a["L0_gnn_W_in1"].T, "W_out1": a["L0_gnn_W_out1"], "W_self1": a["L0_gnn_W_self1"],
        "W_inT2": a["L0_gnn_W_in2"].T, "W_out2": a["L0_gnn_W_out2"], "W_self2": a["L0_gnn_W_self2"],
        "W1": a["L1_gnn_W1"], "W1T": a["L1_gnn_W1"].T, "b": a["L1_gnn_b"],
        "W2": a["L1_gnn_W2"].transpose(1, 0, 2).reshape(D, KM * D),
        "L2_W1": a["L2_gnn_W1"], "L2_W2T": a["L2_gnn_W2"].T, "L2_W3T": a["L2_gnn_W3"].T,
        "U1T": a["L2_gnn_U1"].transpose(0, 2, 1), "U2T": a["L2_gnn_U2"].transpose(0, 2, 1),
        "ln_g": a["L2_gnn_ln_g"], "ln_b": a["L2_gnn_ln_b"], "L3_W": a["L3_gnn_W"], "L3_B": a["L3_gnn_B"],
    }
    for s in ("b_in1", "b_out1", "b_self1", "g1", "be1", "b_in2", "b_out2", "b_self2", "g2", "be2"):
        laid[s] = a["L0_gnn_" + s]
    laid["b_in1"], laid["b_in2"] = laid["b_in1"].reshape(2, P).T, laid["b_in2"].reshape(P, 1)
    nc = bacc.Bacc("TRN2", target_bir_lowering=False, num_devices=1)
    laid = {"in_" + k: np.ascontiguousarray(v) for k, v in laid.items()}
    t = {k[3:]: nc.dram_tensor(k, v.shape, F32, kind="ExternalInput").ap() for k, v in laid.items()}
    out = nc.dram_tensor("out", (N, D), F32, kind="ExternalOutput").ap()
    gnn_kernel(nc, t, out)
    return run(nc, [laid], core_ids=[0]).results[0]["out"]
```

```python
from contextlib import ExitStack

import concourse.bass as bass
from concourse import mybir

F32 = mybir.dt.float32
F16 = mybir.dt.float16
I32 = mybir.dt.int32
ALU = mybir.AluOpType
ACT = mybir.ActivationFunctionType
AX_X = mybir.AxisListType.X

P = 128
N = 2048
NB = N // P
D = 128
H = 256
KM = 16
DA = 64
CH = 512
NCH = N // CH
GRP = 4
NG = NB // GRP
STEPS = 2
EVALS = 6
EARLY = EVALS - GRP
HALVINGS = 40
SEG = 8
WIN = 16

THRESH, EPS, LN_EPS, TOP_P, SUM_MIN = 1e-6, 1e-8, 1e-5, 0.9, 1e-12
M_SCALE = 1024.0
V_SCALE = 64.0
UNSCALE = 1.0 / (M_SCALE * V_SCALE)
R_MIN = 1e-15
ONE_BITS = float(0x3F800000)


def gnn_kernel(nc, t, out):
    with ExitStack() as ctx:
        def sb(name, shape, dt=F32):
            return ctx.enter_context(nc.sbuf_tensor(name, shape, dt))

        big = sb("matrix_parts", [P, 2, NB, N], F16)
        arena = sb("arena", [P, 3 * N])
        s1 = sb("s1", [P, NB * H + 128])
        pa = sb("pa", [P, NB, D])
        pb = sb("pb", [P, NB, D])
        zb = sb("zb", [P, NB, D])
        xb = sb("residual", [P, NB, D])
        wbuf = sb("wbuf", [P, 4 * H + 64])
        ps = ctx.enter_context(nc.psum_tensor("ps", [P, 8 * CH], F32))
        ident = sb("ident", [P, P])
        ones16 = sb("ones16", [P, P], F16)
        lnstats = sb("lnstats", [P, NB, 6])
        lnmean, lndiff, lnvar, lnstd, lninv = (sb(n, [P, NB]) for n in ("lnmean", "lndiff", "lnvar", "lnstd", "lninv"))
        thr_node, wsum, inv_w, no_edge, bias_w, rowsum = (
            sb(n, [P, NB]) for n in ("thr_node", "wsum", "inv_w", "no_edge", "bias_w", "rowsum"))
        minus2, r_min = sb("minus2", [P, 1]), sb("r_min", [P, 1])

        def flat(a):
            return a[:, :, :].rearrange("p b c -> p (b c)")

        def blocks(a, n=NB):
            return a.rearrange("p (b c) -> p b c", b=n)

        def over(col, w, blk=range(NB)):
            return col[:, blk[0]:blk[-1] + 1].unsqueeze(2).to_broadcast([P, len(blk), w])

        def along(row, w, blk=range(NB)):
            return row.unsqueeze(1).to_broadcast([P, len(blk), w])

        HB = NB // 2
        halves = (range(0, HB), range(HB, NB))

        raw = [arena[:, s * N:(s + 1) * N] for s in range(3)]
        tail = arena[:, 2 * N:3 * N]
        pair = s1[:, 0:NB * D].bitcast(F16).rearrange("p (a b c) -> p a b c", a=2, b=NB)
        mask16 = s1[:, NB * D:NB * D + N // 2].bitcast(F16)
        wide = blocks(ps[:, :])
        low4, high4 = blocks(ps[:, 0:N]), blocks(ps[:, N:2 * N])

        hid = blocks(s1[:, 0:NB * H])
        hidT = arena[:, 0:2 * N].rearrange("p (a n) -> p a n", a=2)
        g1, be1, bw1, bo1, bs1 = (tail[:, i * H:(i + 1) * H] for i in range(5))
        g2, be2, bo2, bs2, wout2, bin2_rep = (tail[:, 5 * H + i * D:5 * H + (i + 1) * D] for i in range(6))
        wa1, wself1 = wbuf[:, 0:H], wbuf[:, H:2 * H]
        w2cat = wbuf[:, 2 * H:4 * H].rearrange("p (a c) -> p a c", a=2)
        wtmp = flat(pb)
        winT1 = wtmp[:, 0:256].rearrange("p (a c) -> p a c", a=2)
        wout1 = wtmp[:, 256:768].rearrange("p (a c) -> p a c", a=2)
        winT2 = wtmp[:, 768:1024].rearrange("p (a c) -> p a c", a=2)
        bin1 = wtmp[:, 1024:1026]
        bin2 = wtmp[:, 1026:1027]
        bin1_rep = wtmp[:, 1152:1408].rearrange("p (a c) -> p a c", a=2)
        w2mix = tail
        head_sum = s1[:, KM * D:KM * D + 2 * D].rearrange("p (s c) -> p s c", s=2)
        heads = s1[:, 0:KM * D].rearrange("p (s k c) -> p s k c", s=2, k=KM // 2)
        w1mix = wbuf[:, 0:KM]
        w1mixT = wbuf[0:KM, 16:16 + D]
        bmix = wbuf[0:KM, 144:144 + D]
        w1b = wbuf[:, 272:272 + D]
        node = wbuf[:, 400:400 + NB * KM].rearrange("p (b k) -> p b k", b=NB)
        w1a = wbuf[0:DA, 0:D]
        w2aT = wbuf[0:DA, 128:192]
        w3aT = wbuf[:, 192:256]
        wq = wbuf[:, 256:320]
        u1T = wbuf[:, 320:576].rearrange("p (s c) -> p s c", s=STEPS)
        u2T = wbuf[:, 576:832].rearrange("p (s c) -> p s c", s=STEPS)
        xfT = arena[:, 0:N]
        rawT = arena[:, N:2 * N]
        lng, lnb = wbuf[:, 832:960], wbuf[:, 960:1088]
        qT, kT = s1[0:DA, 0:N], s1[0:DA, N:2 * N]
        att = big[:, :, :, :].rearrange("p a b c -> p (a b c)").bitcast(F32)
        dist = att.rearrange("p (b n) -> p b n", b=NB)
        ahead = {"raw3": (range(0, 6), (arena[:, 0:N], rawT), tail),
                 "raw4": (range(6, 11), (s1[:, 0:N], flat(zb)), arena[:, 0:N]),
                 "raw5": (range(11, NB), (flat(zb), tail), rawT)}
        ebuf = att[:, 0:2 * GRP * N].rearrange("p (g u n) -> p g u n", g=2, u=GRP)
        atT = att[:, 2 * GRP * N:(2 * GRP + 2) * N].rearrange("p (s n) -> p s n", s=2)
        junk = [att[:, (2 * GRP + 2 + i) * N:(2 * GRP + 3 + i) * N] for i in range(3)]
        unread = [att[:, (2 * GRP + 2) * N + u * N // 2:(2 * GRP + 2) * N + (u + 1) * N // 2].bitcast(F16)
                  for u in range(GRP)]
        small_at = [(2 * GRP + 5) * N]

        def small(*shape, dt=F32):
            n = 1
            for k in shape:
                n *= k
            at = small_at[0]
            small_at[0] += (n + 7) // 8 * 8
            v = att[:, at:at + n]
            if dt != F32:
                v = v.bitcast(dt)
            if len(shape) == 2:
                v = v.rearrange("p (a b) -> p a b", a=shape[0])
            if len(shape) == 3:
                v = v.rearrange("p (a b c) -> p a b c", a=shape[0], b=shape[1])
            return v

        negmax, zsum, asum = small(2, GRP), small(2, GRP), small(2, GRP)
        target = [small(GRP) for _ in range(2)]
        bound = [small(2, 2, GRP) for _ in range(2)]
        cand = [small(2, GRP) for _ in range(2)]
        cand_i = [small(GRP, dt=I32) for _ in range(2)]
        cand_f = [c.bitcast(F32) for c in cand_i]
        mass = [small(GRP) for _ in range(2)]
        above, below = small(2, GRP), small(2, GRP)
        width = small(2, GRP)
        frac, t1, t2, t3 = small(GRP), small(GRP), small(GRP), small(GRP)
        seg_top = small(GRP, SEG, 8)
        seg_left = small(GRP, SEG * 8)
        window, csum, dropped, out_vals, kept_vals = (small(GRP, WIN) for _ in range(5))
        cut = small(GRP)
        ones_w = small(WIN)
        act_relu, act_sign = small(GRP), small(GRP)
        goal = [small(GRP) for _ in range(2)]
        act_goal = [small(GRP) for _ in range(2)]
        inv_width, start = small(GRP), small(GRP)
        unread_relu, unread_sign = (small(N // 2).bitcast(F16) for _ in range(2))
        assert small_at[0] <= NB * N

        def half(g, u):
            return N if g == 0 and u % 2 else 0

        def turned_half(g, u):
            return 0 if g == NG - 1 and u % 2 else N
        flags, flagT = small(32), small(32)
        quad = small(4)
        flag_i = small(8, dt=I32)
        gl, gh, gm, gmass, gq = (small(1) for _ in range(5))
        g_up, g_dn = small(1), small(1)

        made = {}

        def sg(name):
            if name not in made:
                made[name] = ctx.enter_context(nc.semaphore(name))
            return made[name]

        DONE = N - GRP * P

        def early(g):
            return EARLY if g else 0

        def sums_before(st, g):
            def sums(groups):
                return sum(2 * (EVALS - early(i)) for i in range(groups)) + 2 * GRP * EARLY * (min(groups, NG - 1))
            return st * sums(NG) + sums(g)

        def slot_uses(s):
            return NB // 3 + (s < NB % 3)

        def each_tile(eng, body):
            with eng.Fori(0, NB // 3) as i:
                for s in range(3):
                    body(i * 3 + s, s, i)
            body(NB - 1, (NB - 1) % 3, NB // 3)

        def stored(n):
            before = [0, 0]
            for tiles, _, _ in ahead.values():
                for m in tiles:
                    slot = (m - tiles[0]) % 2
                    before[slot] += 16
                    if m == n:
                        return sg(f"stored{slot}"), before[slot]

        block = ctx.enter_context(nc.Block())

        @block.sync
        def _(sp):
            def load(dst, src, name):
                sp.dma_start(dst, src).then_inc(sg(name), 16)

            def rows(ap):
                return ap.rearrange("(b p) d -> p b d", p=P)

            def stream(src, turn):
                for s in range(3):
                    if turn:
                        sp.wait_ge(sg(f"raw_free{s}"), slot_uses(s))
                    load(raw[s], src[s * P:(s + 1) * P, :], f"raw_in{s}")
                with sp.Fori(1, NB // 3) as i:
                    for s in range(3):
                        sp.wait_ge(sg(f"raw_free{s}"), i + slot_uses(s) * turn)
                        load(raw[s], src[bass.ds(i * (3 * P) + s * P, P), :], f"raw_in{s}")
                sp.wait_ge(sg("raw_free0"), NB // 3 + slot_uses(0) * turn)
                load(raw[0], src[(NB - 1) * P:NB * P, :], "raw_in0")

            def store_weights(name):
                tiles, bufs, _ = ahead[name]
                for n in tiles:
                    sp.wait_ge(sg("weights"), n + 1)
                    load(t["weights"][n * P:(n + 1) * P, :], bufs[(n - tiles[0]) % 2], f"stored{(n - tiles[0]) % 2}")

            def whole(src, name):
                for s in range(3):
                    load(dist[:, s, :], src[s * P:(s + 1) * P, :], f"{name}{s}")
                with sp.Fori(1, NB // 3) as i:
                    for s in range(3):
                        sp.wait_ge(sg(f"{name}{s}"), i * 16)
                        load(dist[:, i * 3 + s, :], src[bass.ds(i * (3 * P) + s * P, P), :], f"{name}{s}")
                sp.wait_ge(sg(f"{name}0"), NB // 3 * 16)
                load(dist[:, NB - 1, :], src[(NB - 1) * P:NB * P, :], f"{name}0")

            load(xb[:, :, :], rows(t["x"]), "x_in")
            load(winT1, t["W_inT1"].rearrange("(a p) d -> p a d", p=P), "w0_in")
            load(wout1, t["W_out1"].rearrange("(a p) d -> p a d", p=P), "w0_in")
            load(winT2, t["W_inT2"].rearrange("p (a d) -> p a d", a=2), "w0_in")
            load(bin1, t["b_in1"], "w0_in")
            load(bin2, t["b_in2"], "w0_in")
            load(wself1, t["W_self1"], "w0_in")
            load(w2cat[:, :, D:H], t["W_self2"].rearrange("(a p) d -> p a d", p=P), "w0_in")
            stream(t["adj"], 0)
            stream(t["adj"], 1)
            sp.wait_ge(sg("masked"), 1)
            for dst, n in ((g1, "g1"), (be1, "be1"), (bo1, "b_out1"), (bs1, "b_self1"),
                           (g2, "g2"), (be2, "be2"), (bo2, "b_out2"), (bs2, "b_self2")):
                load(dst, t[n].partition_broadcast(P), "vec0_in")
            load(wout2, t["W_out2"], "vec0_in")
            sp.wait_ge(sg("lin2"), 1)
            load(w1mix, t["W1"], "w1_in")
            load(w1mixT, t["W1T"], "w1_in")
            load(bmix, t["b"], "w1_in")
            sp.wait_ge(sg("raw2"), 1)
            whole(t["adjT"], "adjT_in")
            sp.wait_ge(sg("x1"), 1)
            load(w2mix, t["W2"], "w2_in")
            store_weights("raw3")
            sp.wait_ge(sg("x2"), 1)
            load(w1a, t["L2_W1"], "w3_in")
            load(w2aT, t["L2_W2T"], "w3_in")
            load(w3aT, t["L2_W3T"], "w3_in")
            load(u1T, t["U1T"].rearrange("s p c -> p s c"), "w3_in")
            load(u2T, t["U2T"].rearrange("s p c -> p s c"), "w3_in")
            load(lng, t["ln_g"].partition_broadcast(P), "w3_in")
            load(lnb, t["ln_b"].partition_broadcast(P), "w3_in")
            store_weights("raw4")
            store_weights("raw5")
            sp.wait_ge(sg("xa_out"), NB * STEPS)
            load(wbuf[:, 0:D], t["L3_W"], "w4_in")
            load(wbuf[:, D:2 * D], t["L3_B"].partition_broadcast(P), "w4_in")
            for n in (NB - 2, NB - 1):
                sp.wait_ge(*stored(n))
            whole(t["weights"], "dist_in")
            for c in range(NCH):
                some = slice(c * NB // NCH, (c + 1) * NB // NCH)
                sp.wait_ge(sg("x4"), c + 1)
                load(rows(out)[:, some, :], zb[:, some, :], "out_done")
            sp.wait_ge(sg("out_done"), 16 * NCH)

        @block.gpsimd
        def _(pool):
            nc.gpsimd.memset(ident[:, :], 0.0).then_inc(sg("zeroed"), 1)
            pool.wait_ge(sg("zeroed"), 1)
            nc.gpsimd.affine_select(out=ident[:, :], in_=ident[:, :], compare_op=ALU.not_equal, fill=1.0,
                                    base=0, pattern=[[-1, P]], channel_multiplier=1).then_inc(sg("consts"), 1)
            nc.gpsimd.memset(ones16[:, :], 1.0).then_inc(sg("consts"), 1)
            nc.gpsimd.memset(minus2[:, :], -2.0).then_inc(sg("consts"), 1)
            nc.gpsimd.memset(r_min[:, :], R_MIN).then_inc(sg("consts"), 1)

        @block.scalar
        def _(act):
            def root(name, blk=range(NB)):
                act.wait_ge(sg(name + "_var"), 1)
                nc.scalar.activation(lnstd[:, blk[0]:blk[-1] + 1], lnvar[:, blk[0]:blk[-1] + 1],
                                     ACT.Sqrt).then_inc(sg(name + "_std"), 1)

            def copy(dst, src, name, count=1):
                act.wait_ge(sg(name), count)
                nc.scalar.activation(dst, src, ACT.Copy).then_inc(sg(name + "_out"), 1)

            def make_weights(name):
                tiles, bufs, _ = ahead[name]
                nc.scalar.preload_act_table_set("natural_log_exp_and_others")
                for first in tiles[::2]:
                    both = [n for n in (first, first + 1) if n in tiles]
                    for n in both:
                        buf = bufs[(n - tiles[0]) % 2]
                        if n - 2 in tiles:
                            act.wait_ge(*stored(n - 2))
                        elif name == "raw5" and n == first:
                            act.wait_ge(*stored(ahead["raw4"][0][-2]))
                        nc.scalar.activation(buf, dist[:, n, :], ACT.Ln, bias=r_min[:, 0:1]).then_inc(sg("ln_r"), 1)
                        act.wait_ge(sg("ln_r"), n + 1)
                        nc.scalar.activation(buf, buf, ACT.Exp, scale=-1.0).then_inc(sg("inverse"), 1)
                    for n in both:
                        buf = bufs[(n - tiles[0]) % 2]
                        act.wait_ge(sg("neg_inverse"), n + 1)
                        if n == first:
                            nc.scalar.activation(buf, buf, ACT.Exp, scale=-2.0, bias=minus2[:, 0:1]).then_inc(
                                sg("sens"), 1)
                        else:
                            nc.scalar.activation(buf, buf, ACT.Square, bias=1.0).then_inc(sg("sens_sq"), 1)
                            act.wait_ge(sg("sens_sq"), squares.index(n) + 1)
                            nc.scalar.activation(buf, buf, ACT.Exp, scale=-2.0).then_inc(sg("sens"), 1)

            squares = [n for tiles, _, _ in ahead.values() for n in tiles[1::2]]

            def split_high():
                def tile(n, s, i):
                    act.wait_ge(sg(f"raw_in{s}"), i * 16 + 16)
                    nc.scalar.activation(big[:, 0, n, :], raw[s], ACT.Copy, scale=M_SCALE,
                                         accum_out=rowsum[:, bass.ds(n, 1)]).then_inc(sg("high_adj"), 1)

                each_tile(act, tile)

            root("ln0")
            split_high()
            copy(arena[:, 0:N], ps[:, 0:N], "raw1")
            act.wait_ge(sg("wprod"), 1)
            nc.scalar.activation(wa1, ps[:, N:N + H], ACT.Copy).then_inc(sg("wprod_out"), 1)
            nc.scalar.activation(w2cat[:, :, 0:D], ps[:, N + CH:N + CH + H].rearrange("p (a c) -> p a c", a=2),
                                 ACT.Copy).then_inc(sg("wprod_out"), 1)
            nc.scalar.activation(bw1, ps[:, N + 2 * CH:N + 2 * CH + H], ACT.Copy).then_inc(sg("wprod_out"), 1)
            copy(flat(pb), ps[:, N:2 * N], "h0T")
            copy(arena[:, 0:N], ps[:, 0:N], "uT")
            for h in range(2):
                root(f"ln1_{h}", halves[h])
                for a in range(2):
                    copy(hidT[:, a, h * HB * P:(h + 1) * HB * P], ps[:, h * N + a * HB * P:h * N + (a + 1) * HB * P],
                         "hidT", h * 2 + a + 1)
            copy(arena[:, 0:N], ps[:, 0:N], "raw2")
            root("ln2")
            root("ln3")
            copy(flat(pb), ps[:, 0:N], "h1T")
            copy(w1b, ps[:, N:N + D], "w1b")
            copy(node, ps[:, N + CH:N + CH + NB * KM].rearrange("p (b k) -> p b k", b=NB), "node")
            with act.Fori(0, NB // 2) as i:
                for s in range(2):
                    b = i * 2 + s
                    act.wait_ge(sg("mix_mm"), b + 1)
                    act.wait_ge(sg(("mix_even", "mix_odd")[s]), i + 1)
                    for k in range(KM // 2):
                        o = s * N + (KM // 2 + k) * D
                        ins = nc.scalar.activation(heads[:, s, k, :], ps[:, o:o + D], ACT.Copy,
                                                   scale=node[:, b, KM // 2 + k:KM // 2 + k + 1])
                    ins.then_inc(sg("mix_scaled"), 1)
            for s in range(3):
                act.wait_ge(sg(f"adjT_in{s}"), 16 * slot_uses(s))
            make_weights("raw3")
            for c in range(NCH):
                bank = slice(c * CH, (c + 1) * CH)
                act.wait_ge(sg("raw3"), c + 1)
                nc.scalar.activation(s1[:, bank], ps[:, bank], ACT.Relu).then_inc(sg("raw3_out"), 1)
            copy(wq, ps[:, 7 * CH:7 * CH + DA], "wq")
            root("ln4")
            make_weights("raw4")
            act.wait_ge(*stored(ahead["raw3"][0][-1]))
            for c in range(NCH):
                copy(rawT[:, c * CH:(c + 1) * CH], ps[:, c * CH:(c + 1) * CH], "raw4", c + 1)
            copy(tail, ps[:, 0:N], "xaT")
            act.wait_ge(*stored(ahead["raw4"][0][-1]))
            copy(qT, ps[0:DA, 0:N], "qT")
            copy(kT, ps[0:DA, 0:N], "kT")
            copy(xfT, ps[:, N:2 * N], "xf1T")
            make_weights("raw5")
            copy(rawT, ps[:, 0:N], "raw5", NCH)
            for st in range(STEPS):
                xT = (pb, pa)[st]

                def exps(g, u):
                    n = st * NB + g * GRP + u
                    act.wait_ge(sg("rowmax"), n + 1)
                    if g >= 2:
                        act.wait_ge(sg("a_turned"), n - 2 * GRP + 1)
                    o = half(g, u)
                    nc.scalar.activation(ebuf[:, g % 2, u, :], ps[:, o:o + N], ACT.Exp, bias=negmax[:, g % 2, u:u + 1],
                                         accum_out=zsum[:, g % 2, u:u + 1]).then_inc(sg("e_ready"), 1)

                def turned(g, u):
                    n = st * NB + g * GRP + u
                    act.wait_ge(sg("a_turned"), n + 1)
                    if n >= 2:
                        act.wait_ge(sg("ax"), n - 1)
                    o = turned_half(g, u)
                    nc.scalar.activation(atT[:, n % 2, :], ps[:, o:o + N], ACT.Copy).then_inc(sg("at_out"), 1)

                def mixed(g, u):
                    n = st * NB + g * GRP + u
                    act.wait_ge(sg("ax"), n + 1)
                    if u == 0:
                        act.wait_ge(sg("a_sums"), st * NG + g + 1)
                    o = turned_half(g, u)
                    nc.scalar.activation(xT[:, g * GRP + u, :], ps[:, o:o + D], ACT.Copy,
                                         scale=asum[:, g % 2, u:u + 1]).then_inc(sg("xa_out"), 1)

                def evaluate(g, k):
                    act.wait_ge(sg("candidate"), (st * NG + g) * (EVALS + 1) + k + 1)
                    relu_and_sign(g, GRP - 1)

                def relu_and_sign(g, u):
                    e, t = ebuf[:, g % 2, u, :], cand_f[g % 2][:, u:u + 1]
                    nc.scalar.activation(unread_relu, e, ACT.Relu, scale=-1.0, bias=t,
                                         accum_out=act_relu[:, u:u + 1]).then_inc(sg("act_sums"), 1)
                    nc.scalar.activation(unread_sign, e, ACT.Sign, scale=-1.0, bias=t,
                                         accum_out=act_sign[:, u:u + 1]).then_inc(sg("act_sums"), 1)

                def evaluate_early(g, k):
                    done = sums_before(st, g) - 2 * GRP * (EARLY - k)
                    act.wait_ge(sg("candidate"), (st * NG + g) * (EVALS + 1) + k + 1)
                    for u in range(GRP):
                        if u:
                            act.wait_ge(sg("act_sums"), done + 2 * u)
                        relu_and_sign(g, u)

                for u in range(GRP):
                    exps(0, u)
                for g in range(NG):
                    for k in range(EVALS - early(g)):
                        evaluate(g, k + early(g))
                        if g >= 1 and k < GRP:
                            turned(g - 1, k)
                        if g + 1 < NG and k < GRP:
                            exps(g + 1, k)
                        if g >= 1 and k < GRP:
                            mixed(g - 1, k)
                    if g + 1 < NG:
                        for k in range(EARLY):
                            evaluate_early(g + 1, k)
                if st == 0:
                    copy(tail[:, 0:DONE], ps[:, 0:DONE], "x_first")
                    copy(qT[:, 0:DONE], ps[0:DA, N:N + DONE], "q_first")
                    copy(kT[:, 0:DONE], ps[0:DA, 0:DONE], "k_first")
                turned(NG - 1, 0)
                for u in range(GRP):
                    if u + 1 < GRP:
                        turned(NG - 1, u + 1)
                    mixed(NG - 1, u)
                if st == 0:
                    copy(tail[:, DONE:N], ps[:, 0:CH], "x_rest")
                    copy(qT[:, DONE:N], ps[0:DA, N:N + CH], "q_rest")
                    copy(kT[:, DONE:N], ps[0:DA, N + CH:N + 2 * CH], "k_rest")
            copy(flat(pb), ps[:, 0:N], "xaT", 2)
            root("ln5")
            root("ln6")
            copy(flat(pb), ps[:, 0:N], "h3T")
            for c in range(NCH):
                copy(flat(pb)[:, c * CH:(c + 1) * CH], ps[:, c * CH:(c + 1) * CH], "x4T", c + 1)

        @block.tensor
        def _(pe):
            def turn(src, col0, name):
                for b in range(NB):
                    mm = nc.tensor.transpose(ps[:, col0 + b * P:col0 + (b + 1) * P], src[:, b, :], ident[:, :])
                mm.then_inc(sg(name), 1)

            def linear(srcT, w, col0, name):
                for b in range(NB):
                    mm = nc.tensor.matmul(ps[:, col0 + b * P:col0 + (b + 1) * P], flat(srcT)[:, b * P:(b + 1) * P], w,
                                          start=True, stop=True)
                mm.then_inc(sg(name), 1)

            def tile_fp16(j, first, last):
                for c in range(NCH):
                    for n, (a, w) in enumerate(((0, 0), (0, 1), (1, 0))):
                        mm = nc.tensor.matmul(ps[:, c * CH:(c + 1) * CH], pair[:, w, j, :],
                                              big[:, a, j, c * CH:(c + 1) * CH],
                                              start=first and n == 0, stop=last and n == 2)
                return mm

            def product(vec, name, first=True):
                for j in range(NB):
                    for c in range(NCH):
                        mm = nc.tensor.matmul(ps[:, c * CH:(c + 1) * CH], vec[:, j, :], dist[:, j, c * CH:(c + 1) * CH],
                                              start=first and j == 0, stop=j == NB - 1)
                        if j == NB - 1:
                            mm.then_inc(sg(name), 1)

            def turn_back(src, raw_name, name):
                for c in range(NCH):
                    pe.wait_ge(sg(raw_name + "_out"), c + 1)
                    for b in range(c * NB // NCH, (c + 1) * NB // NCH):
                        mm = nc.tensor.transpose(ps[:, N + b * P:N + (b + 1) * P], src[:, b, :], ident[:, :])
                mm.then_inc(sg(name), 1)

            pe.wait_ge(sg("consts"), 4)
            def colsum_tile(n, s, i):
                pe.wait_ge(sg(f"raw_free{s}"), i + 1)
                for c in range(NCH):
                    for a in range(2):
                        mm = nc.tensor.matmul(ps[:, (c + 4 * a) * CH:(c + 4 * a + 1) * CH], ones16[:, :],
                                              big[:, a, n, c * CH:(c + 1) * CH], start=False, stop=False,
                                              skip_group_check=True)
                mm.then_inc(sg("colsum_mm"), 1)

            each_tile(pe, colsum_tile)
            pe.wait_ge(sg("thresholds"), 1)
            pe.wait_ge(sg("h0_pair"), 1)

            def tile1(j, first=False, last=False):
                pe.wait_ge(sg("mask_mul"), j * 2 + 2)
                tile_fp16(j, first, last)
                for c in range(NCH):
                    for a in range(2):
                        mm = nc.tensor.matmul(ps[:, (c + 4) * CH:(c + 5) * CH], ones16[:, :],
                                              big[:, a, j, c * CH:(c + 1) * CH],
                                              start=first and a == 0, stop=last and a == 1)
                return mm

            tile1(0, first=True)
            with pe.Fori(1, NB - 1) as j:
                tile1(j)
            tile1(NB - 1, last=True).then_inc(sg("raw1"), 1)
            pe.wait_ge(sg("raw1_out"), 1)
            turn(blocks(arena[:, 0:N]), 0, "prod1")
            pe.wait_ge(sg("w_read"), 1)
            pe.wait_ge(sg("w0_in"), 16 * 7)
            pe.wait_ge(sg("vec0_in"), 16 * 9)
            pe.wait_ge(sg("bin_rep"), 1)
            for a in range(2):
                nc.tensor.matmul(ps[:, N:N + H], winT1[:, a, :], wout1[:, a, :], start=(a == 0), stop=(a == 1))
            for a in range(2):
                nc.tensor.matmul(ps[:, N + CH + a * D:N + CH + (a + 1) * D], winT2[:, a, :], wout2,
                                 start=True, stop=True)
            for a in range(2):
                mm = nc.tensor.matmul(ps[:, N + 2 * CH:N + 2 * CH + H], bin1_rep[:, a, :], wout1[:, a, :],
                                      start=(a == 0), stop=(a == 1))
            mm.then_inc(sg("wprod"), 1)
            pe.wait_ge(sg("wprod_out"), 3)
            turn(pa, N, "h0T")
            pe.wait_ge(sg("u"), 1)
            turn(zb, 0, "uT")
            pe.wait_ge(sg("h0T_out"), 1)
            pe.wait_ge(sg("uT_out"), 1)
            for blk in halves:
                for b in blk:
                    o = ps[:, b * H:(b + 1) * H]
                    nc.tensor.matmul(o, arena[:, b * P:(b + 1) * P], wa1, start=True, stop=False)
                    mm = nc.tensor.matmul(o, flat(pb)[:, b * P:(b + 1) * P], wself1, start=False, stop=True)
                mm.then_inc(sg("lin1"), 1)
            for h, blk in enumerate(halves):
                pe.wait_ge(sg("hid"), h + 1)
                for a in range(2):
                    for b in blk:
                        o = h * N + (a * HB + b - blk[0]) * P
                        mm = nc.tensor.transpose(ps[:, o:o + P], hid[:, b, a * P:(a + 1) * P], ident[:, :])
                    mm.then_inc(sg("hidT"), 1)
                pe.wait_ge(sg("hidT_out"), 2 * (h + 1))
                for b in blk:
                    o = ps[:, b * H:(b + 1) * H]
                    nc.tensor.matmul(o, hidT[:, 0, b * P:(b + 1) * P], w2cat[:, 0, :], start=True, stop=False)
                    nc.tensor.matmul(ps[:, b * H:b * H + D], bin2_rep, wout2, start=False, stop=False)
                    mm = nc.tensor.matmul(o, hidT[:, 1, b * P:(b + 1) * P], w2cat[:, 1, :], start=False, stop=True)
                mm.then_inc(sg("lin2"), 1)
            pe.wait_ge(sg("p_pair"), 2)
            tile_fp16(0, True, False)
            with pe.Fori(1, NB - 1) as j:
                tile_fp16(j, False, False)
            tile_fp16(NB - 1, False, True).then_inc(sg("raw2"), 1)
            pe.wait_ge(sg("raw2_out"), 1)
            turn(blocks(arena[:, 0:N]), N, "prod2")
            pe.wait_ge(sg("h1"), 1)
            turn(pa, 0, "h1T")
            pe.wait_ge(sg("w1_in"), 16 * 3)
            nc.tensor.matmul(ps[:, N:N + D], w1mixT, bmix, start=True, stop=True).then_inc(sg("w1b"), 1)
            pe.wait_ge(sg("h1T_out"), 1)
            for b in range(NB):
                mm = nc.tensor.matmul(ps[:, N + CH + b * KM:N + CH + (b + 1) * KM], flat(pb)[:, b * P:(b + 1) * P],
                                      w1mix, start=True, stop=True)
            mm.then_inc(sg("node"), 1)
            pe.wait_ge(sg("w1b_out"), 1)
            pe.wait_ge(sg("node_out"), 1)
            pe.wait_ge(sg("w2_in"), 16)
            for b in range(NB):
                if b >= 2:
                    pe.wait_ge(sg("mix_used"), b - 1)
                    pe.wait_ge(sg("mix_scaled"), b - 1)
                for c in range(NCH):
                    o = (b % 2 * NCH + c) * CH
                    mm = nc.tensor.matmul(ps[:, o:o + CH], flat(pb)[:, b * P:(b + 1) * P],
                                          w2mix[:, c * CH:(c + 1) * CH], start=True, stop=True)
                mm.then_inc(sg("mix_mm"), 1)
            pe.wait_ge(sg("mix_used"), NB)
            for c in range(NCH):
                nc.tensor.matmul(ps[:, c * CH:(c + 1) * CH], w1b, flat(pb)[:, c * CH:(c + 1) * CH],
                                 start=True, stop=False)
            pe.wait_ge(sg("y"), 1)
            for s in range(3):
                pe.wait_ge(sg(f"adjT_in{s}"), 16 * (NB // 3 + (s < NB % 3)))
            product(zb, "raw3", first=False)
            turn_back(blocks(s1[:, 0:N]), "raw3", "prod3")
            pe.wait_ge(sg("w3_in"), 16 * 7)
            pe.wait_ge(sg("x2"), 1)
            nc.tensor.matmul(ps[:, 7 * CH:7 * CH + DA], w1a, w2aT, start=True, stop=True).then_inc(sg("wq"), 1)
            pe.wait_ge(sg("h2"), 1)
            product(pa, "raw4")
            pe.wait_ge(sg("wq_out"), 1)
            turn_back(blocks(rawT), "raw4", "prod4")
            turn(pa, 0, "xaT")
            pe.wait_ge(sg("xaT_out"), 1)
            for w, name in ((wq, "qT"), (w3aT, "kT")):
                for c in range(NCH):
                    mm = nc.tensor.matmul(ps[0:DA, c * CH:(c + 1) * CH], w, tail[:, c * CH:(c + 1) * CH],
                                          start=True, stop=True)
                mm.then_inc(sg(name), 1)
                pe.wait_ge(sg(name + "_out"), 1)
            pe.wait_ge(sg("xf1"), 1)
            turn(pb, N, "xf1T")
            product(pb, "raw5")
            pe.wait_ge(sg("xf1T_out"), 1)
            for b in range(NB):
                mm = nc.tensor.matmul(ps[:, N + b * P:N + (b + 1) * P], xfT[:, b * P:(b + 1) * P], u1T[:, 0, :],
                                      start=True, stop=True)
            mm.then_inc(sg("zxf1"), 1)
            for st in range(STEPS):
                xa, xT = ((pa, pb), (pb, pa))[st]

                def logits(g, u):
                    n = st * NB + g * GRP + u
                    if g == 0 and u >= 2:
                        pe.wait_ge(sg("e_ready"), n - 1)
                    if g:
                        pe.wait_ge(sg("e_ready"), n)
                    for c in range(NCH):
                        o = half(g, u) + c * CH
                        mm = nc.tensor.matmul(ps[:, o:o + CH], qT[:, (g * GRP + u) * P:(g * GRP + u + 1) * P],
                                              kT[:, c * CH:(c + 1) * CH], start=True, stop=True)
                    mm.then_inc(sg("logits"), 1)

                def turn_a(g, u):
                    n = st * NB + g * GRP + u
                    if g == 0 and u == 0:
                        pe.wait_ge(sg("z_xa1" if st else "z_xf2"), 1)
                    pe.wait_ge(sg("a_masked"), n + 1)
                    if g == NG - 1 and u >= 2:
                        pe.wait_ge(sg("xa_out"), n - 1)
                    elif n and turned_half(g, u):
                        pe.wait_ge(sg("xa_out"), n)
                    for j in range(NB):
                        o = turned_half(g, u) + j * P
                        mm = nc.tensor.transpose(ps[:, o:o + P], ebuf[:, g % 2, u, j * P:(j + 1) * P], ident[:, :])
                    mm.then_inc(sg("a_turned"), 1)

                def mix_a(g, u):
                    n = st * NB + g * GRP + u
                    pe.wait_ge(sg("at_out"), n + 1)
                    o = turned_half(g, u)
                    for j in range(NB):
                        mm = nc.tensor.matmul(ps[:, o:o + D], atT[:, n % 2, j * P:(j + 1) * P], xa[:, j, :],
                                              start=(j == 0), stop=(j == NB - 1))
                    mm.then_inc(sg("ax"), 1)

                if st == 0:
                    pe.wait_ge(sg("raw5_out"), 1)
                logits(0, 0)
                if st == 0:
                    pe.wait_ge(sg("z_xf1"), 1)
                    for b in range(NB):
                        o = ps[:, N + b * P:N + (b + 1) * P]
                        nc.tensor.matmul(o, rawT[:, b * P:(b + 1) * P], u1T[:, 1, :], start=True, stop=False)
                        mm = nc.tensor.matmul(o, xfT[:, b * P:(b + 1) * P], u1T[:, 1, :], start=False, stop=True)
                    mm.then_inc(sg("zxf2"), 1)
                    pe.wait_ge(sg("z_xf2"), 1)
                for u in range(1, GRP):
                    logits(0, u)
                if st:
                    pe.wait_ge(sg("e_ready"), NB * st + GRP)
                    for b in range(NB):
                        mm = nc.tensor.matmul(ps[:, N + b * P:N + (b + 1) * P], tail[:, b * P:(b + 1) * P],
                                              u2T[:, 0, :], start=True, stop=True)
                    mm.then_inc(sg("zxa1"), 1)
                for g in range(NG):
                    for u in range(GRP):
                        if g >= 1:
                            turn_a(g - 1, u)
                        if g + 1 < NG:
                            logits(g + 1, u)
                        if g >= 1:
                            mix_a(g - 1, u)

                def projections(b0, cols, q0, k0, name):
                    for i in range(cols // P):
                        mm = nc.tensor.transpose(ps[:, i * P:(i + 1) * P], xT[:, b0 + i, :], ident[:, :])
                    mm.then_inc(sg("x" + name), 1)
                    pe.wait_ge(sg("x" + name + "_out"), 1)
                    for w, o, which in ((wq, q0, "q"), (w3aT, k0, "k")):
                        for c in range(cols // CH):
                            at = b0 * P + c * CH
                            mm = nc.tensor.matmul(ps[0:DA, o + c * CH:o + (c + 1) * CH], w, tail[:, at:at + CH],
                                                  start=True, stop=True)
                        mm.then_inc(sg(which + name), 1)
                    pe.wait_ge(sg("q" + name + "_out"), 1)
                    pe.wait_ge(sg("k" + name + "_out"), 1)

                if st == 0:
                    pe.wait_ge(sg("xa_out"), NB - GRP)
                    pe.wait_ge(sg("e_ready"), NB)
                    projections(0, DONE, N, 0, "_first")
                turn_a(NG - 1, 0)
                for u in range(GRP):
                    if u + 1 < GRP:
                        turn_a(NG - 1, u + 1)
                    mix_a(NG - 1, u)
                pe.wait_ge(sg("xa_out"), NB * (st + 1))
                if st == 0:
                    projections(NB - GRP, N - DONE, N, N + CH, "_rest")
            turn(pa, 0, "xaT")
            pe.wait_ge(sg("xaT_out"), 2)
            linear(pb, u2T[:, 1, :], N, "zxa2")
            pe.wait_ge(sg("h3"), 1)
            turn(pa, 0, "h3T")
            pe.wait_ge(sg("h3T_out"), 1)
            pe.wait_ge(sg("w4_in"), 16 * 2)
            linear(pb, wbuf[:, 0:D], N, "msg")
            pe.wait_ge(sg("msg_b"), 1)
            for j in range(NB):
                pe.wait_ge(sg(f"dist_in{j % 3}"), 16 * (j // 3 + 1))
                for c in range(NCH):
                    mm = nc.tensor.matmul(ps[:, c * CH:(c + 1) * CH], zb[:, j, :], dist[:, j, c * CH:(c + 1) * CH],
                                          start=(j == 0), stop=(j == NB - 1))
                    if j == NB - 1:
                        mm.then_inc(sg("x4T"), 1)
            for c in range(NCH):
                pe.wait_ge(sg("x4T_out"), c + 1)
                for b in range(c * NB // NCH, (c + 1) * NB // NCH):
                    mm = nc.tensor.transpose(ps[:, N + b * P:N + (b + 1) * P], pb[:, b, :], ident[:, :])
                mm.then_inc(sg("prod6"), 1)

        @block.vector
        def _(dve):
            v = nc.vector
            done = [0]

            def step(ins):
                ins.then_inc(sg("dve_step"), 1)
                done[0] += 1
                dve.wait_ge(sg("dve_step"), done[0])

            def tell(ins, name, count=1):
                ins.then_inc(sg(name), 1)
                dve.wait_ge(sg(name), count)

            def layernorm(src, dst, w, name, gamma=None, beta=None, relu=True, blk=range(NB)):
                some = slice(blk[0], blk[-1] + 1)
                mean, diff, var = lnmean[:, some], lndiff[:, some], lnvar[:, some]
                for b in blk:
                    v.bn_stats(lnstats[:, b, :], src[:, b, :])
                dve.drain()
                v.tensor_tensor(mean, lnstats[:, some, 1], lnstats[:, some, 4], ALU.add)
                v.tensor_tensor(diff, lnstats[:, some, 1], lnstats[:, some, 4], ALU.subtract)
                v.tensor_tensor(var, lnstats[:, some, 2], lnstats[:, some, 5], ALU.add)
                dve.drain()
                v.tensor_scalar(mean, mean, 0.5, None, ALU.mult)
                v.tensor_tensor(diff, diff, diff, ALU.mult)
                v.tensor_scalar(var, var, 1.0 / w, LN_EPS, ALU.mult, ALU.add)
                dve.drain()
                tell(v.scalar_tensor_tensor(out=var, in0=diff, scalar=0.25, in1=var,
                                            op0=ALU.mult, op1=ALU.add), name + "_var")
                dve.wait_ge(sg(name + "_std"), 1)
                step(v.reciprocal(lninv[:, some], lnstd[:, some]))
                for b in blk:
                    v.tensor_scalar(dst[:, b, :], src[:, b, :], lnmean[:, b:b + 1], lninv[:, b:b + 1],
                                    ALU.subtract, ALU.mult)
                dve.drain()
                dst = dst[:, some, :]
                if gamma is not None:
                    step(v.tensor_tensor(dst, dst, along(gamma, w, blk), ALU.mult))
                    step(v.tensor_tensor(dst, dst, along(beta, w, blk), ALU.add))
                if relu:
                    step(v.tensor_scalar(dst, dst, 0.0, None, ALU.max))

            def make_pair(src, name):
                step(v.tensor_scalar(pair[:, 0, :, :], src, V_SCALE, None, ALU.mult))
                tell(v.scalar_tensor_tensor(out=pair[:, 1, :, :], in0=src, scalar=V_SCALE, in1=pair[:, 0, :, :],
                                            op0=ALU.mult, op1=ALU.subtract), name)

            def make_weights(name):
                tiles, bufs, ratio = ahead[name]
                for first in tiles[::2]:
                    both = [n for n in (first, first + 1) if n in tiles]
                    for n in both:
                        buf = bufs[(n - tiles[0]) % 2]
                        dve.wait_ge(sg("inverse"), n + 1)
                        v.tensor_tensor(ratio, dist[:, n, :], buf, ALU.mult)
                        dve.drain()
                        ins = v.scalar_tensor_tensor(out=buf, in0=ratio, scalar=-2.0, in1=buf, op0=ALU.add,
                                                     op1=ALU.mult)
                        if n == first:
                            dve.drain()
                            ins = v.scalar_tensor_tensor(out=buf, in0=buf, scalar=2.0, in1=buf, op0=ALU.add,
                                                         op1=ALU.mult)
                        ins.then_inc(sg("neg_inverse"), 1)
                        dve.drain()
                    for n in both:
                        buf = bufs[(n - tiles[0]) % 2]
                        dve.wait_ge(sg("sens"), n + 1)
                        v.scalar_tensor_tensor(out=buf, in0=dist[:, n, :], scalar=1.0, in1=buf,
                                               op0=ALU.is_lt, op1=ALU.mult).then_inc(sg("weights"), 1)

            def split_low():
                def tile(n, s, i):
                    dve.wait_ge(sg("high_adj"), n + 1)
                    v.scalar_tensor_tensor(out=big[:, 1, n, :], in0=raw[s], scalar=M_SCALE, in1=big[:, 0, n, :],
                                           op0=ALU.mult, op1=ALU.subtract).then_inc(sg(f"raw_free{s}"), 1)

                each_tile(dve, tile)

            marker = [sb(f"marker{s}", [P, 1]) for s in range(2)]

            step(v.memset(ps[:, :], 0.0))
            dve.wait_ge(sg("x_in"), 16)
            layernorm(xb[:, :, :], pa[:, :, :], D, "ln0")
            make_pair(pa[:, :, :], "h0_pair")
            split_low()
            dve.wait_ge(sg("w0_in"), 16 * 7)
            thr = flat(zb)
            dve.wait_ge(sg("colsum_mm"), NB)
            step(v.tensor_scalar(thr, ps[:, 0:N], THRESH / M_SCALE, THRESH * EPS, ALU.mult, ALU.add))
            tell(v.scalar_tensor_tensor(out=thr, in0=ps[:, N:2 * N], scalar=THRESH / M_SCALE, in1=thr,
                                        op0=ALU.mult, op1=ALU.add), "thresholds")

            def mask_tile(n, s, i):
                dve.wait_ge(sg(f"raw_in{s}"), i * 16 + 16 * (slot_uses(s) + 1))
                v.tensor_tensor(mask16, raw[s], thr, ALU.is_gt).then_inc(sg(f"raw_free{s}"), 1)
                dve.wait_ge(sg(f"raw_free{s}"), i + (slot_uses(s) + 1))
                for a in range(2):
                    m = big[:, a, n, :]
                    v.tensor_tensor(m, m, mask16, ALU.mult).then_inc(sg("mask_mul"), 1)
                dve.wait_ge(sg("mask_mul"), n * 2 + 2)

            each_tile(dve, mask_tile)
            for a in range(2):
                step(v.tensor_scalar(bin1_rep[:, a, :], zb[:, 0, :], 0.0, bin1[:, a:a + 1], ALU.mult, ALU.add))
            tell(v.memset(marker[0][:, :], 0.0), "masked")
            tell(v.tensor_scalar(bin2_rep, zb[:, 0, :], 0.0, bin2, ALU.mult, ALU.add), "bin_rep")
            dve.wait_ge(sg("consts"), 4)
            step(v.tensor_tensor(blocks(rawT), zb[:, :, :], along(ident[:, :], D), ALU.mult))
            step(v.tensor_reduce(thr_node[:, :], blocks(rawT), AX_X, ALU.add))
            dve.wait_ge(sg("raw1"), 1)
            step(v.tensor_tensor(zb[:, :, :], high4, along(ident[:, :], D), ALU.mult))
            tell(v.tensor_reduce(wsum[:, :], zb[:, :, :], AX_X, ALU.add), "w_read")
            step(v.tensor_scalar(wsum[:, :], wsum[:, :], 1.0 / M_SCALE, None, ALU.mult))
            step(v.tensor_scalar(no_edge[:, :], wsum[:, :], 0.0, None, ALU.is_le))
            step(v.scalar_tensor_tensor(out=inv_w[:, :], in0=thr_node[:, :], scalar=EPS / THRESH, in1=wsum[:, :],
                                        op0=ALU.mult, op1=ALU.add))
            step(v.reciprocal(inv_w[:, :], inv_w[:, :]))
            step(v.tensor_tensor(bias_w[:, :], wsum[:, :], inv_w[:, :], ALU.mult))
            step(v.tensor_tensor(bias_w[:, :], bias_w[:, :], no_edge[:, :], ALU.add))
            step(v.tensor_scalar(inv_w[:, :], inv_w[:, :], UNSCALE, None, ALU.mult))
            step(v.tensor_tensor(zb[:, :, :], pa[:, :, :], over(no_edge[:, :], D), ALU.mult))
            dve.wait_ge(sg("prod1"), 1)
            step(v.tensor_tensor(blocks(rawT), low4, over(inv_w[:, :], D), ALU.mult))
            tell(v.tensor_tensor(zb[:, :, :], zb[:, :, :], blocks(rawT), ALU.add), "u")
            dve.wait_ge(sg("vec0_in"), 16 * 9)
            dve.wait_ge(sg("wprod_out"), 3)
            step(v.tensor_tensor(bo1, bo1, bs1, ALU.add))
            step(v.tensor_tensor(bo2, bo2, bs2, ALU.add))
            step(v.tensor_tensor(hid, along(bw1, H), over(bias_w[:, :], H), ALU.mult))
            step(v.tensor_tensor(hid, hid, along(bo1, H), ALU.add))
            for h, blk in enumerate(halves):
                some = slice(blk[0], blk[-1] + 1)
                dve.wait_ge(sg("lin1"), h + 1)
                step(v.tensor_tensor(hid[:, some, :], hid[:, some, :], wide[:, some, :], ALU.add))
                layernorm(hid, hid, H, f"ln1_{h}", g1, be1, blk=blk)
                tell(v.memset(marker[h][:, :], 0.0), "hid", h + 1)
            for h, blk in enumerate(halves):
                some = slice(blk[0], blk[-1] + 1)
                dve.wait_ge(sg("lin2"), h + 1)
                p = wide[:, some, 0:D]
                v.tensor_scalar(pair[:, 0, some, :], p, V_SCALE, None, ALU.mult)
                v.tensor_tensor(zb[:, some, :], wide[:, some, D:H], along(bo2, D, blk), ALU.add)
                v.tensor_tensor(pb[:, some, :], p, over(no_edge, D, blk), ALU.mult)
                dve.drain()
                v.scalar_tensor_tensor(out=pair[:, 1, some, :], in0=p, scalar=V_SCALE, in1=pair[:, 0, some, :],
                                       op0=ALU.mult, op1=ALU.subtract).then_inc(sg("p_pair"), 1)
            dve.drain()
            step(v.tensor_tensor(zb[:, :, :], zb[:, :, :], pb[:, :, :], ALU.add))
            dve.wait_ge(sg("prod2"), 1)
            step(v.tensor_tensor(pa[:, :, :], high4, over(inv_w[:, :], D), ALU.mult))
            step(v.tensor_tensor(pa[:, :, :], pa[:, :, :], zb[:, :, :], ALU.add))
            layernorm(pa[:, :, :], pa[:, :, :], D, "ln2", g2, be2)
            tell(v.tensor_tensor(xb[:, :, :], xb[:, :, :], pa[:, :, :], ALU.add), "x1")
            layernorm(xb[:, :, :], pa[:, :, :], D, "ln3")
            tell(v.memset(marker[0][:, :], 0.0), "h1")
            dve.wait_ge(sg("node_out"), 1)
            for s in range(2):
                v.memset(marker[s][:, :], 0.0).then_inc(sg(("mix_even", "mix_odd")[s]), 1)
            with dve.Fori(0, NB // 2) as i:
                for s in range(2):
                    b = i * 2 + s
                    dve.wait_ge(sg("mix_mm"), b + 1)
                    for k in range(KM // 2):
                        o = s * N + k * D
                        src, w = ps[:, o:o + D], node[:, b, k:k + 1]
                        if k == 0:
                            ins = v.tensor_scalar(zb[:, b, :], src, w, None, ALU.mult)
                        else:
                            ins = v.scalar_tensor_tensor(out=zb[:, b, :], in0=src, scalar=w, in1=zb[:, b, :],
                                                         op0=ALU.mult, op1=ALU.add)
                        ins.then_inc(sg("mix_used" if k == KM // 2 - 1 else "mix_add"), 1)
                        if k < KM // 2 - 1:
                            dve.wait_ge(sg("mix_add"), b * (KM // 2 - 1) + (k + 1))
                    dve.wait_ge(sg("mix_scaled"), b + 1)
                    v.tensor_reduce(head_sum[:, s, :], heads[:, s, :, :].rearrange("p k c -> p c k"), AX_X,
                                    ALU.add).then_inc(sg(("mix_even", "mix_odd")[s]), 1)
                    dve.drain()
                    v.tensor_tensor(zb[:, b, :], zb[:, b, :], head_sum[:, s, :], ALU.add)
            dve.drain()
            tell(v.memset(marker[1][:, :], 0.0), "y")
            make_weights("raw3")
            dve.wait_ge(sg("prod3"), 1)
            tell(v.tensor_tensor(xb[:, :, :], high4, xb[:, :, :], ALU.add), "x2")
            layernorm(xb[:, :, :], pa[:, :, :], D, "ln4")
            tell(v.memset(marker[0][:, :], 0.0), "h2")
            step(v.tensor_scalar(wsum[:, :], rowsum[:, :], 1.0 / M_SCALE, 1.0, ALU.mult, ALU.add))
            step(v.reciprocal(wsum[:, :], wsum[:, :]))
            make_weights("raw4")
            dve.wait_ge(sg("prod4"), 1)
            step(v.tensor_tensor(pb[:, :, :], high4, pa[:, :, :], ALU.add))
            tell(v.tensor_tensor(pb[:, :, :], pb[:, :, :], over(wsum[:, :], D), ALU.mult), "xf1")
            make_weights("raw5")
            dve.wait_ge(sg("zxf1"), 1)
            dve.wait_ge(*stored(NB - 1))
            dve.wait_ge(*stored(NB - 2))
            tell(v.tensor_tensor(zb[:, :, :], pa[:, :, :], high4, ALU.add), "z_xf1")
            step(v.memset(ones_w, 1.0))
            step(v.memset(flags, 0.0))

            def bc2(a):
                return a.unsqueeze(1).to_broadcast([P, 2, GRP])

            def row_max(st, g, u, n_const, k):
                dve.wait_ge(sg("logits"), k + (n_const + 1))
                o = 0 if u is None else half(g, u)
                v.tensor_reduce(negmax[:, g % 2, bass.ds(k, 1)] if u is None else negmax[:, g % 2, u:u + 1],
                                ps[:, o:o + N], AX_X, ALU.max, negate=True).then_inc(sg("rowmax"), 1)

            def update(p, to):
                bd, cd = bound[p], cand[p]
                v.tensor_tensor(cd[:, 1, :], mass[p], to, ALU.subtract)
                dve.drain()
                v.tensor_scalar(above, bc2(cd[:, 1, :]), 0.0, None, ALU.is_ge)
                v.tensor_scalar(below, bc2(cd[:, 1, :]), 0.0, None, ALU.is_lt)
                dve.drain()
                v.copy_predicated(bd[:, 0, :, :], above.bitcast(I32), cd)
                v.copy_predicated(bd[:, 1, :, :], below.bitcast(I32), cd)
                dve.drain()
                v.tensor_tensor(width, bd[:, 1, :, :], bd[:, 0, :, :], ALU.subtract)
                v.scalar_tensor_tensor(out=frac, in0=cand_f[p], scalar=-6.0, in1=bd[:, 0, 1, :],
                                       op0=ALU.mult, op1=ALU.subtract)
                dve.drain()
                v.reciprocal(inv_width, width[:, 1, :])
                dve.drain()
                v.tensor_tensor(frac, frac, inv_width, ALU.mult)
                dve.drain()
                v.tensor_scalar(frac, frac, 0.98, 0.02, ALU.min, ALU.max)
                dve.drain()
                v.tensor_tensor(frac, frac, width[:, 0, :], ALU.mult)
                dve.drain()
                v.tensor_tensor(cand_i[p], frac, bd[:, 0, 0, :], ALU.add).then_inc(sg("candidate"), 1)
                v.tensor_tensor(cd[:, 0, :], frac, bd[:, 0, 0, :], ALU.add)
                dve.drain()

            def update_early(st, g, k):
                p = g % 2
                dve.wait_ge(sg("act_sums"), sums_before(st, g) - 2 * GRP * (EARLY - 1 - k))
                v.tensor_scalar(act_sign, act_sign, -0.5, -0.5 * N, ALU.mult, ALU.add)
                v.tensor_scalar(bound[p][:, :, 1, :], bound[p][:, :, 1, :], 0.7, None, ALU.mult)
                dve.drain()
                v.tensor_tensor(mass[p], cand_f[p], act_sign, ALU.mult)
                dve.drain()
                v.tensor_tensor(mass[p], mass[p], act_relu, ALU.add)
                dve.drain()
                update(p, act_goal[p])

            def begin(st, g):
                p = g % 2
                dve.wait_ge(sg("e_ready"), st * NB + (g + 1) * GRP)
                zs = zsum[:, p, :]
                v.tensor_scalar(target[p], zs, TOP_P, None, ALU.mult)
                v.tensor_scalar(start, zs, 0.0999 / N, None, ALU.mult)
                v.memset(bound[p][:, 1, 0, :], ONE_BITS)
                v.tensor_scalar(goal[p][:, 0:GRP - 1], zs[:, 0:GRP - 1], TOP_P - 1e-5, None, ALU.mult)
                v.tensor_scalar(goal[p][:, GRP - 1:GRP], zs[:, GRP - 1:GRP], TOP_P - 3e-5 - 1.0, None, ALU.mult)
                v.tensor_scalar(act_goal[p], zs, TOP_P - 3e-5 - 1.0, None, ALU.mult)
                dve.drain()
                v.tensor_copy(bound[p][:, 0, 0, :], start.bitcast(I32))
                v.tensor_tensor(bound[p][:, 0, 1, :], zs, target[p], ALU.subtract)
                v.tensor_scalar(bound[p][:, 1, 1, :], target[p], -1.0, None, ALU.mult)
                dve.drain()
                v.tensor_scalar(cand[p][:, 0, :], bound[p][:, 0, 0, :], 0.75, 0.25 * ONE_BITS, ALU.mult, ALU.add)
                dve.drain()
                v.tensor_copy(cand_i[p], cand[p][:, 0, :]).then_inc(sg("candidate"), 1)
                dve.drain()

            def evaluations(g, count, sums, produce):
                p = g % 2
                with dve.Fori(0, count) as k:
                    for u in range(GRP - 1):
                        e = ebuf[:, p, u, :]
                        v.scalar_tensor_tensor(out=unread[u], in0=e, scalar=cand_f[p][:, u:u + 1], in1=e,
                                               op0=ALU.is_gt, op1=ALU.mult, accum_out=mass[p][:, u:u + 1])
                    if produce is not None:
                        row_max(None, g + 1, None, produce, k)
                    dve.wait_ge(sg("act_sums"), k * 2 + (sums + 2))
                    v.tensor_scalar(act_sign, act_sign, -0.5, -0.5 * N, ALU.mult, ALU.add)
                    dve.drain()
                    v.scalar_tensor_tensor(out=mass[p][:, GRP - 1:GRP], in0=cand_f[p][:, GRP - 1:GRP],
                                           scalar=act_sign[:, GRP - 1:GRP], in1=act_relu[:, GRP - 1:GRP],
                                           op0=ALU.mult, op1=ALU.add)
                    v.tensor_scalar(bound[p][:, :, 1, :], bound[p][:, :, 1, :], 0.7, None, ALU.mult)
                    dve.drain()
                    update(p, goal[p])

            def general(g):
                with dve.Fori(0, GRP) as u:
                    e = ebuf[:, g % 2, u, :]
                    tg, zs = target[g % 2][:, bass.ds(u, 1)], zsum[:, g % 2, bass.ds(u, 1)]
                    v.tensor_scalar(gl, zs, 0.0999 / N, None, ALU.mult)
                    v.memset(gh, 1.0)
                    v.memset(gmass, 0.0)
                    dve.drain()
                    with dve.Fori(0, HALVINGS) as _:
                        v.tensor_scalar(gm, gl, gh[:, 0:1], 0.5, ALU.add, ALU.mult)
                        dve.drain()
                        v.scalar_tensor_tensor(out=junk[0], in0=e, scalar=gm[:, 0:1], in1=e, op0=ALU.is_gt, op1=ALU.mult,
                                               accum_out=gq)
                        dve.drain()
                        v.tensor_tensor(g_up, gq, tg, ALU.is_ge)
                        v.tensor_tensor(g_dn, gq, tg, ALU.is_lt)
                        dve.drain()
                        v.copy_predicated(gl, g_up.bitcast(I32), gm)
                        v.copy_predicated(gh, g_dn.bitcast(I32), gm)
                        v.copy_predicated(gmass, g_dn.bitcast(I32), gq)
                        dve.drain()
                    v.tensor_tensor(gq, tg, gmass, ALU.subtract)
                    v.reciprocal(gm, gh)
                    v.tensor_scalar(junk[0], e, gh[:, 0:1], None, ALU.is_equal)
                    v.memset(junk[1], 1.0)
                    dve.drain()
                    v.tensor_scalar(gq, gq, gm[:, 0:1], 1.0, ALU.mult, ALU.add)
                    v.tensor_tensor_scan(junk[2], junk[1], junk[0], 0.0, ALU.mult, ALU.add)
                    dve.drain()
                    v.scalar_tensor_tensor(out=junk[0], in0=junk[2], scalar=gq[:, 0:1], in1=junk[0],
                                           op0=ALU.is_lt, op1=ALU.mult)
                    dve.drain()
                    v.scalar_tensor_tensor(out=junk[0], in0=e, scalar=gh[:, 0:1], in1=junk[0],
                                           op0=ALU.is_gt, op1=ALU.add)
                    dve.drain()
                    v.scalar_tensor_tensor(out=e, in0=e, scalar=1.0, in1=junk[0], op0=ALU.mult, op1=ALU.mult,
                                           accum_out=asum[:, g % 2, bass.ds(u, 1)]).then_inc(sg("a_masked"), 1)
                    dve.drain()

            def search(st, g):
                base = st * NB + g * GRP
                p = g % 2
                zs = zsum[:, p, :]
                if g == 0:
                    begin(st, g)
                sums = sums_before(st, g)
                evaluations(g, GRP, sums, base + GRP if g + 1 < NG else None)
                if g == 0:
                    if st:
                        dve.wait_ge(sg("zxa1"), 1)
                        tell(v.tensor_tensor(zb[:, :, :], zb[:, :, :], high4, ALU.add), "z_xa1")
                    evaluations(g, EVALS - GRP, sums + 2 * GRP, None)
                step(v.tensor_copy(cand_i[p], bound[p][:, 1, 0, :]))
                for u in range(GRP):
                    e = ebuf[:, g % 2, u, :]
                    v.scalar_tensor_tensor(out=junk[u % 2], in0=e, scalar=cand_f[p][:, u:u + 1], in1=e,
                                           op0=ALU.is_le, op1=ALU.mult, accum_out=mass[p][:, u:u + 1])
                    if u == 0 and g + 1 < NG:
                        begin(st, g + 1)
                    dve.drain()
                    for q in range(SEG):
                        v.max(seg_top[:, u, q, :], junk[u % 2][:, q * (N // SEG):(q + 1) * (N // SEG)])
                if g + 1 < NG:
                    for k in range(EARLY - 1):
                        update_early(st, g + 1, k)
                dve.drain()
                for u in range(GRP):
                    v.max(window[:, u, 0:8], seg_top[:, u, :, :].rearrange("p s c -> p (s c)"))
                dve.drain()
                for u in range(GRP):
                    v.match_replace(seg_left[:, u, :], window[:, u, 0:8],
                                    seg_top[:, u, :, :].rearrange("p s c -> p (s c)"), 0.0)
                v.tensor_tensor(t1, zs, mass[p], ALU.subtract)
                dve.drain()
                for u in range(GRP):
                    v.max(window[:, u, 8:WIN], seg_left[:, u, :])
                dve.drain()
                for u in range(GRP):
                    v.tensor_tensor_scan(csum[:, u, :], ones_w, window[:, u, :], t1[:, u:u + 1], ALU.mult, ALU.add)
                dve.drain()
                step(v.tensor_tensor(csum, csum, window, ALU.subtract))
                step(v.tensor_tensor(dropped, csum, target[p].unsqueeze(2).to_broadcast([P, GRP, WIN]), ALU.is_ge))
                v.tensor_tensor(out_vals, dropped, window, ALU.mult)
                v.scalar_tensor_tensor(out=kept_vals, in0=dropped, scalar=2.0, in1=window, op0=ALU.mult, op1=ALU.add)
                v.scalar_tensor_tensor(out=t3, in0=dropped[:, :, 0], scalar=1.0, in1=dropped[:, :, WIN - 1],
                                       op0=ALU.add, op1=ALU.subtract)
                v.tensor_reduce(t1, seg_top[:, :, :, 7], AX_X, ALU.max)
                dve.drain()
                v.tensor_reduce(t2, out_vals, AX_X, ALU.max)
                v.tensor_reduce(cut, kept_vals, AX_X, ALU.min)
                dve.drain()
                step(v.tensor_tensor(t2, t2, t1, ALU.max))
                step(v.tensor_tensor(t2, t2, cut, ALU.is_ge))
                step(v.tensor_tensor(t2, t2, t3, ALU.add))
                step(v.tensor_reduce(flags[:, 0:1], t2, AX_X, ALU.max))
                step(v.transpose(flagT, flags))
                step(v.tensor_reduce(t3[:, 0:1], flagT, AX_X, ALU.max))
                for q in range(4):
                    v.tensor_copy(quad[0:1, q:q + 1], t3[32 * q:32 * q + 1, 0:1])
                dve.drain()
                step(v.tensor_reduce(flag_i[0:1, 0:1], quad[0:1, :], AX_X, ALU.max))
                if st * NG + g >= 2:
                    dve.wait_ge(sg("xa_out"), base - GRP)
                undecided = dve.value_load(flag_i[0:1, 0:1], min_val=0, max_val=4)
                with dve.If(undecided > 0):
                    general(g)
                with dve.Else():
                    for u in range(GRP):
                        e = ebuf[:, g % 2, u, :]
                        v.scalar_tensor_tensor(out=e, in0=e, scalar=cut[:, u:u + 1], in1=e, op0=ALU.is_ge,
                                               op1=ALU.mult,
                                               accum_out=asum[:, g % 2, u:u + 1]).then_inc(sg("a_masked"), 1)
                    dve.drain()
                step(v.tensor_scalar(asum[:, g % 2, :], asum[:, g % 2, :], SUM_MIN, None, ALU.max))
                tell(v.reciprocal(asum[:, g % 2, :], asum[:, g % 2, :]), "a_sums", st * NG + g + 1)
                if g + 1 < NG:
                    update_early(st, g + 1, EARLY - 1)

            for st in range(STEPS):
                row_max(st, 0, 0, st * NB, 0)
                if st == 0:
                    dve.wait_ge(sg("zxf2"), 1)
                    step(v.tensor_tensor(pb[:, :, :], high4, over(wsum[:, :], D), ALU.mult))
                    tell(v.tensor_tensor(zb[:, :, :], zb[:, :, :], pb[:, :, :], ALU.add), "z_xf2")
                for u in range(1, GRP):
                    row_max(st, 0, u, st * NB + u, 0)
                for g in range(NG):
                    search(st, g)
            dve.wait_ge(sg("zxa2"), 1)
            step(v.tensor_tensor(zb[:, :, :], zb[:, :, :], high4, ALU.add))
            layernorm(zb[:, :, :], zb[:, :, :], D, "ln5", lng, lnb, relu=False)
            tell(v.tensor_tensor(xb[:, :, :], xb[:, :, :], zb[:, :, :], ALU.add), "x3")
            layernorm(xb[:, :, :], pa[:, :, :], D, "ln6")
            tell(v.memset(marker[0][:, :], 0.0), "h3")
            dve.wait_ge(sg("w4_in"), 16 * 2)
            dve.wait_ge(sg("msg"), 1)
            tell(v.tensor_tensor(zb[:, :, :], high4, along(wbuf[:, D:2 * D], D), ALU.add), "msg_b")

            for c in range(NCH):
                some = slice(c * NB // NCH, (c + 1) * NB // NCH)
                dve.wait_ge(sg("prod6"), c + 1)
                v.tensor_tensor(zb[:, some, :], high4[:, some, :], xb[:, some, :], ALU.add).then_inc(sg("x4"), 1)


def kernel(**inputs):
    import numpy as np
    import concourse.bacc as bacc
    from concourse.bass_utils import run_bass_kernel_spmd as run

    a = {k: np.asarray(v) for k, v in inputs.items()}
    laid = {
        "x": a["x"], "adj": a["adj"], "adjT": a["adj"].T,
        "W_inT1": a["L0_gnn_W_in1"].T, "W_out1": a["L0_gnn_W_out1"], "W_self1": a["L0_gnn_W_self1"],
        "W_inT2": a["L0_gnn_W_in2"].T, "W_out2": a["L0_gnn_W_out2"], "W_self2": a["L0_gnn_W_self2"],
        "W1": a["L1_gnn_W1"], "W1T": a["L1_gnn_W1"].T, "b": a["L1_gnn_b"],
        "W2": a["L1_gnn_W2"].transpose(1, 0, 2).reshape(D, KM * D),
        "L2_W1": a["L2_gnn_W1"], "L2_W2T": a["L2_gnn_W2"].T, "L2_W3T": a["L2_gnn_W3"].T,
        "U1T": a["L2_gnn_U1"].transpose(0, 2, 1), "U2T": a["L2_gnn_U2"].transpose(0, 2, 1),
        "ln_g": a["L2_gnn_ln_g"], "ln_b": a["L2_gnn_ln_b"], "L3_W": a["L3_gnn_W"], "L3_B": a["L3_gnn_B"],
    }
    for s in ("b_in1", "b_out1", "b_self1", "g1", "be1", "b_in2", "b_out2", "b_self2", "g2", "be2"):
        laid[s] = a["L0_gnn_" + s]
    laid["b_in1"], laid["b_in2"] = laid["b_in1"].reshape(2, P).T, laid["b_in2"].reshape(P, 1)
    nc = bacc.Bacc("TRN2", target_bir_lowering=False, num_devices=1)
    laid = {"in_" + k: np.ascontiguousarray(v) for k, v in laid.items()}
    t = {k[3:]: nc.dram_tensor(k, v.shape, F32, kind="ExternalInput").ap() for k, v in laid.items()}
    t["weights"] = nc.dram_tensor("layer3_weights", (N, N), F32, kind="Internal").ap()
    out = nc.dram_tensor("out", (N, D), F32, kind="ExternalOutput").ap()
    gnn_kernel(nc, t, out)
    return run(nc, [laid], core_ids=[0]).results[0]["out"]
```
